# Optimizing a Trainium2 kernel written in Bass

```python
import numpy as np
import jax
import jax.numpy as jnp

def _softmax(x, axis=-1):
    return jax.nn.softmax(x, axis=axis)

def _gelu(x):
    return jax.nn.gelu(x, approximate=True)

def _silu(x):
    return jax.nn.silu(x)

def _sigmoid(x):
    return jax.nn.sigmoid(x)

def _layernorm(x, axis=-1, eps=1e-05):
    m = jnp.mean(x, axis=axis, keepdims=True)
    v = jnp.var(x, axis=axis, keepdims=True)
    return (x - m) / jnp.sqrt(v + eps)

def _scatter_add(tgt, idx, src, axis=0):
    return tgt.at[idx].add(src)

def _segment_sum(src, seg, n):
    return jax.ops.segment_sum(src, seg, n)
kernel_name = 'mk_gnn_resnorm_d2_gnn_r8_7613c3'

def setup_inputs(seed: int=0):
    np.random.seed(seed)
    _w = jnp.asarray

    def _rec_inputs():
        import jax
        import jax.numpy as jnp
        _gk = jax.random.key(seed)
        x = -0.0009044 + 1 * jax.random.normal(jax.random.fold_in(_gk, 1), (12500, 32), jnp.float32)
        _s = jax.random.randint(jax.random.fold_in(_gk, 2), (100000,), 0, 12500, jnp.int32)
        _d = jax.random.randint(jax.random.fold_in(_gk, 3), (100000,), 0, 12500, jnp.int32)
        _loop = jnp.arange(12500, dtype=jnp.int32)
        src = jnp.concatenate([_s, _d, _loop])
        dst = jnp.concatenate([_d, _s, _loop])
        _o = jnp.argsort(dst, stable=True)
        src = src[_o]
        dst = dst[_o]
        edge_attr_32 = 0.000196303 + 1.00016 * jax.random.normal(jax.random.fold_in(_gk, 12), (212500, 32), jnp.float32)
        edge_type_86 = jax.random.randint(jax.random.fold_in(_gk, 14), (212500,), 0, 86, jnp.int32)
        return (x, src, dst, edge_attr_32, edge_type_86)
    x, src, dst, edge_attr_32, edge_type_86 = _rec_inputs()

    def _L0_gnn_setup():
        import jax, jax.numpy as jnp
        import numpy as np
        N_NODES = 6250
        N_EDGES = 100000
        X_DIM = 32
        E_DIM = 32
        HID = 64
        OUT = 32
        key = jax.random.key(seed)
        ks = jax.random.split(key, 6)
        x = jax.random.normal(ks[0], (N_NODES, X_DIM), dtype=jnp.float32)
        edge_index = jax.random.randint(ks[1], (2, N_EDGES), 0, N_NODES, dtype=jnp.int64)
        edge_attr = jax.random.normal(ks[2], (N_EDGES, E_DIM), dtype=jnp.float32)
        in_dim = 2 * X_DIM + E_DIM
        W1 = jax.random.normal(ks[3], (in_dim, HID), dtype=jnp.float32) * (1.0 / np.sqrt(in_dim))
        b1 = jnp.zeros((HID,), dtype=jnp.float32)
        W2 = jax.random.normal(ks[4], (HID, OUT), dtype=jnp.float32) * (1.0 / np.sqrt(HID))
        b2 = jnp.zeros((OUT,), dtype=jnp.float32)
        return {'x': x, 'edge_index': edge_index, 'edge_attr': edge_attr, 'W1': W1, 'b1': b1, 'W2': W2, 'b2': b2}
    _L0_gnn_all = _L0_gnn_setup()
    _L0_gnn_in = {k: v for k, v in _L0_gnn_all.items() if k in ('W1', 'b1', 'W2', 'b2')}
    del _L0_gnn_all

    def _L1_gnn_setup():
        import jax, jax.numpy as jnp
        import numpy as np
        N_NODES = 6250
        N_EDGES = 100000
        INP_DIM = 32
        OUT_DIM = 32
        ATTN_DIM = 32
        NUM_RELS = 86
        NUM_BASES = 16
        GAMMA = 0.0
        key = jax.random.key(seed)
        ks = jax.random.split(key, 12)
        return {'h': jax.random.normal(ks[0], (N_NODES, INP_DIM), jnp.float32), 'weight': jax.random.normal(ks[1], (NUM_BASES, INP_DIM, OUT_DIM), jnp.float32), 'w_comp': jax.random.normal(ks[2], (NUM_RELS, NUM_BASES), jnp.float32), 'self_loop_weight': jax.random.normal(ks[3], (INP_DIM, OUT_DIM), jnp.float32), 'A1_w': jax.random.normal(ks[4], (ATTN_DIM, INP_DIM), jnp.float32), 'A1_b': jax.random.normal(ks[5], (ATTN_DIM,), jnp.float32), 'A2_w': jax.random.normal(ks[6], (ATTN_DIM, INP_DIM), jnp.float32), 'A2_b': jax.random.normal(ks[7], (ATTN_DIM,), jnp.float32), 'rel_emb': jax.random.normal(ks[8], (NUM_RELS, ATTN_DIM), jnp.float32), 'src': jax.random.randint(ks[9], (N_EDGES,), 0, N_NODES, jnp.int32), 'dst': jax.random.randint(ks[10], (N_EDGES,), 0, N_NODES, jnp.int32), 'etype': jax.random.randint(ks[11], (N_EDGES,), 0, NUM_RELS, jnp.int32)}
    _L1_gnn_all = _L1_gnn_setup()
    _L1_gnn_in = {k: v for k, v in _L1_gnn_all.items() if k in ('weight', 'w_comp', 'self_loop_weight', 'A1_w', 'A1_b', 'A2_w', 'A2_b', 'rel_emb')}
    del _L1_gnn_all
    return {'x': x, 'src': src, 'dst': dst, 'edge_attr_32': edge_attr_32, 'edge_type_86': edge_type_86, 'L0_gnn_W1': _L0_gnn_in['W1'], 'L0_gnn_b1': _L0_gnn_in['b1'], 'L0_gnn_W2': _L0_gnn_in['W2'], 'L0_gnn_b2': _L0_gnn_in['b2'], 'L1_gnn_weight': _L1_gnn_in['weight'], 'L1_gnn_w_comp': _L1_gnn_in['w_comp'], 'L1_gnn_self_loop_weight': _L1_gnn_in['self_loop_weight'], 'L1_gnn_A1_w': _L1_gnn_in['A1_w'], 'L1_gnn_A1_b': _L1_gnn_in['A1_b'], 'L1_gnn_A2_w': _L1_gnn_in['A2_w'], 'L1_gnn_A2_b': _L1_gnn_in['A2_b'], 'L1_gnn_rel_emb': _L1_gnn_in['rel_emb']}

def reference(x, src, dst, edge_attr_32, edge_type_86, L0_gnn_W1, L0_gnn_b1, L0_gnn_W2, L0_gnn_b2, L1_gnn_weight, L1_gnn_w_comp, L1_gnn_self_loop_weight, L1_gnn_A1_w, L1_gnn_A1_b, L1_gnn_A2_w, L1_gnn_A2_b, L1_gnn_rel_emb):
    import jax
    import jax.numpy as jnp

    def _L0_gnn_ref(x, edge_index, edge_attr, W1, b1, W2, b2):
        import jax, jax.numpy as jnp
        import numpy as np
        N_NODES = 6250
        N_EDGES = 100000
        X_DIM = 32
        E_DIM = 32
        HID = 64
        OUT = 32
        num_nodes = x.shape[0]
        rol, col = (edge_index[0], edge_index[1])
        e_feat = jnp.concatenate([x[rol], x[col], edge_attr], axis=-1)
        h = jax.nn.relu(e_feat @ W1 + b1)
        v = h @ W2 + b2
        x_cand = jax.ops.segment_max(v, col, num_segments=num_nodes)
        return jnp.maximum(x_cand, x[:, -v.shape[-1]:])

    def _L1_gnn_ref(h, weight, w_comp, self_loop_weight, A1_w, A1_b, A2_w, A2_b, rel_emb, src, dst, etype):
        import jax, jax.numpy as jnp
        import numpy as np
        N_NODES = 6250
        N_EDGES = 100000
        INP_DIM = 32
        OUT_DIM = 32
        ATTN_DIM = 32
        NUM_RELS = 86
        NUM_BASES = 16
        GAMMA = 0.0
        E = src.shape[0]
        N = h.shape[0]
        x = h[src]
        y = h[dst]
        c = w_comp[etype]
        xb = jnp.einsum('ei,bio->ebo', x, weight)
        msg = jnp.einsum('eb,ebo->eo', c, xb)
        x_hat = x @ A1_w.T + A1_b
        y_hat = y @ A2_w.T + A2_b + rel_emb[etype]
        scale = jnp.sqrt(jnp.asarray(INP_DIM, h.dtype))
        a = jnp.tanh(jax.nn.relu(jnp.sum(x_hat * y_hat, axis=-1) / scale))
        a = jnp.where(a > GAMMA, a, jnp.zeros_like(a))
        nei = jax.ops.segment_sum(a[:, None] * msg, dst, num_segments=N)
        last_e = jax.ops.segment_max(jnp.arange(E, dtype=jnp.int32), dst, num_segments=N)
        last_e = jnp.clip(last_e, 0, E - 1)
        curr = h[src[last_e]] @ self_loop_weight
        in_deg = jax.ops.segment_sum(jnp.ones((E,), h.dtype), dst, num_segments=N)
        h_new = jnp.where((in_deg > 0)[:, None], nei + curr, jnp.zeros_like(nei))
        return jax.nn.relu(h_new)
    edge_index = jnp.stack([src, dst])
    x = _layernorm(x + _L0_gnn_ref(x, edge_index, edge_attr_32, L0_gnn_W1, L0_gnn_b1, L0_gnn_W2, L0_gnn_b2), axis=-1)
    x = _layernorm(x + _L1_gnn_ref(x, L1_gnn_weight, L1_gnn_w_comp, L1_gnn_self_loop_weight, L1_gnn_A1_w, L1_gnn_A1_b, L1_gnn_A2_w, L1_gnn_A2_b, L1_gnn_rel_emb, src, dst, edge_type_86), axis=-1)
    return x

_drawn_inputs = setup_inputs


def setup_inputs(seed=0):
    import zlib

    import numpy as np

    out = dict(_drawn_inputs(seed))
    spreads = {'L0_gnn_b1': (0.0, 0.1), 'L0_gnn_b2': (0.0, 0.1)}
    factors = {}
    for name, (base, spread) in spreads.items():
        noise = np.random.default_rng([zlib.crc32(name.encode()), seed]).standard_normal(out[name].shape)
        drawn = base * np.exp(spread * noise) if base else spread * noise
        out[name] = jnp.asarray(drawn.astype(out[name].dtype))
    for name, factor in factors.items():
        out[name] = (out[name] * factor).astype(out[name].dtype)
    return out
```

```python
from contextlib import ExitStack

import numpy as np

import concourse.bass as bass
from concourse import mybir

P = 128
N_NODES, N_EDGES = 12500, 212500
F = 32
HID = 64
BASES = 16
STREAMS = 4
LEN = 512
TILES = LEN // P
SLOTS = STREAMS * TILES
STEPS = -(-N_EDGES // (STREAMS * LEN))
STEPS += STEPS % 2
STREAM = STEPS * LEN
EDGES = STREAMS * STREAM
ROW = EDGES // P
NODE_COLS = -(-N_NODES // P)
NODES = P * NODE_COLS
CHUNK = 14
CHUNKS = NODE_COLS // CHUNK
GROUPS = [(a, min(a + 4, CHUNK)) for a in range(0, CHUNK, 4)]
BLOCK = 512
BLOCKS = EDGES // BLOCK
SEARCH = 10
SEARCHES = -(-(NODE_COLS + 1) // SEARCH)
PARTS = 3
KCH = BASES // 4
BIG = 3.0e38
EPS = 1e-5
C_BANKS = 3
G_BUFS = 8

fp32, bf16, i32 = mybir.dt.float32, mybir.dt.bfloat16, mybir.dt.int32
ALU = mybir.AluOpType
ACT = mybir.ActivationFunctionType
AX = mybir.AxisListType


def bc(ap, shape, axis):
    return ap.unsqueeze(axis).broadcast_to(shape)


def build(nc, t):
    ctx = ExitStack()
    with ctx:
        def sb(name, shape, dt=fp32):
            return ctx.enter_context(nc.sbuf_tensor(name, shape, dt))

        def dram(name, shape, dt=fp32):
            return nc.dram_tensor(name, shape, dt, kind="Internal").ap()

        def sem(name):
            return ctx.enter_context(nc.semaphore(name))

        dst_blocks = dram("dst_blocks", [BLOCKS, BLOCK])
        keep_dram = dram("keep_dram", [EDGES], bf16)
        type_dram = dram("type_dram", [EDGES], bf16)
        spread = dram("spread", [EDGES + NODES, F])
        max_rows = dram("max_rows", [EDGES, F])
        sum_rows = dram("sum_rows", [EDGES, 2 * F])
        h_dram = dram("h_dram", [NODES, 4 * F])
        y_dram = dram("y_dram", [NODES, F])

        ident = sb("ident", [P, P])
        w1 = sb("w1", [P, 3, 2, P])
        w2 = sb("w2", [P, 2, P])
        b1 = sb("b1", [P, 1])
        b2 = sb("b2", [P, F])
        a1w = sb("a1w", [P, F])
        a1b = sb("a1b", [P, 1])
        a2w = sb("a2w", [P, P])
        a2b = sb("a2b", [P, F])
        self_w = sb("self_w", [P, P])
        basis = sb("basis", [P, KCH, F])
        ones_blk = sb("ones_blk", [P, P])
        sel_f = sb("sel_f", [P, 2 * KCH, P])
        sel = sb("sel", [P, 2 * KCH, P], bf16)
        rel = sb("rel", [P, F + BASES])
        rest = sb("rest", [P, F + BASES])
        rest2 = sb("rest2", [P, F + BASES])
        rel_parts = sb("rel_parts", [P, PARTS, F + BASES], bf16)
        comp_lhs = sb("comp_lhs", [P, 64], bf16)
        row_id = sb("row_id", [P, 1])
        node_id = sb("node_id", [P, NODE_COLS + 1])
        spare_id = sb("spare_id", [P, NODE_COLS])
        eps = sb("eps", [P, 1])

        x = sb("x", [P, NODE_COLS, F])
        early = sb("early", [P, 3 * NODE_COLS * F])
        h = early[:, 0:NODE_COLS * F].rearrange("p (t f) -> p t f", f=F)
        y = early[:, NODE_COLS * F:2 * NODE_COLS * F].rearrange("p (t f) -> p t f", f=F)
        agg = early[:, 2 * NODE_COLS * F:].rearrange("p (t f) -> p t f", f=F)
        dst_i = early[:, 0:ROW].bitcast(i32)
        prev_i = early[:, ROW:2 * ROW].bitcast(i32)
        type_i = early[:, 2 * ROW:3 * ROW].bitcast(i32)
        dst_f = early[:, 3 * ROW:4 * ROW]
        keep_b = early[:, 4 * ROW:4 * ROW + ROW // 2].bitcast(bf16)
        type_b = early[:, 4 * ROW + ROW // 2:5 * ROW].bitcast(bf16)
        heads_i = sb("heads_i", [P, BLOCKS], i32)
        heads = sb("heads", [P, BLOCKS])
        below = sb("below", [P, 2, BLOCK], bf16)
        block_f = sb("block_f", [P, NODE_COLS + 1])
        block_i = sb("block_i", [P, NODE_COLS + 1], i32)
        inside = sb("inside", [P, NODE_COLS + 1])
        first = sb("first", [P, NODE_COLS + 1])
        last = sb("last", [P, NODE_COLS])
        last_i = sb("last_i", [P, NODE_COLS], i32)
        has = sb("has", [P, NODE_COLS])
        no_edge = sb("no_edge", [P, NODE_COLS])
        place = sb("place", [P, NODE_COLS])
        past = sb("past", [P, NODE_COLS])
        place_i = sb("place_i", [P, NODE_COLS], i32)
        crosses = sb("crosses", [P, STREAMS, NODE_COLS])
        crosses2 = sb("crosses2", [P, STREAMS, NODE_COLS])
        no_cross = sb("no_cross", [P, STREAMS, NODE_COLS])
        border = sb("border", [P, STREAMS, F])
        heads4 = sb("heads4", [STREAMS, 1], i32)
        rows4 = sb("rows4", [STREAMS, F])
        node_a = sb("node_a", [P, CHUNK, F])
        node_b = sb("node_b", [P, CHUNK, F])
        node_c = sb("node_c", [P, CHUNK, F])
        stat_a = sb("stat_a", [P, CHUNK])
        stat_b = sb("stat_b", [P, CHUNK])
        stat_c = sb("stat_c", [P, CHUNK])
        node_t = sb("node_t", [P, 4 * P])
        last_rows = sb("last_rows", [P, 2, CHUNK, 2 * F])

        src_idx = sb("src_idx", [P, 2, SLOTS], i32)
        xg = sb("xg", [P, 2, SLOTS, 4 * F])
        xg0 = xg[:, :, 0:SLOTS // 4, :].rearrange("p u k (c f) -> p u (k c) f", f=F)
        ea = sb("ea", [P, 2, LEN])
        sp_in = sb("sp_in", [P, 2, SLOTS, F])
        keep = sb("keep", [P, 2, LEN], bf16)
        fresh = sb("fresh", [P, 2, LEN], bf16)
        xt = sb("xt", [P, 2, LEN])
        dt_ = sb("dt_", [P, 2, LEN])
        hid = sb("hid", [P, 2, 2, LEN])
        scan = sb("scan", [P, 2, LEN])
        out0 = sb("out0", [P, 2, SLOTS, F])
        late = sb("late", [P, 15 * 1024])
        at = [0]

        def part(n):
            at[0] += n
            return late[:, at[0] - n:at[0]]
        x4 = part(2 * STREAMS * LEN).rearrange("p (u g n) -> p u g n", u=2, g=STREAMS)
        prod = part(G_BUFS * LEN).rearrange("p (b n) -> p b n", b=G_BUFS)
        types = part(STREAMS * LEN).bitcast(bf16).rearrange("p (u g n) -> p u g n", u=2, g=STREAMS)
        onehot = part(STREAMS * LEN).bitcast(bf16).rearrange("p (u g n) -> p u g n", u=2, g=STREAMS)
        out1 = part(2 * SLOTS * 2 * F).rearrange("p (u k f) -> p u k f", u=2, k=SLOTS)
        rows = late[:, 0:2 * SEARCH * BLOCK].rearrange("p (u t n) -> p u t n", u=2, t=SEARCH)
        ZERO = 4096
        zero = late[:, 15 * 1024 - ZERO:15 * 1024]
        comp = sb("comp", [P, 2, LEN], bf16)
        query, score, weight, wmsg = (hid[:, k // 2, k % 2, :] for k in range(4))

        bank = [ctx.enter_context(nc.psum_tensor(f"bank{i}", [P, 512], fp32)) for i in range(8)]

        loaded = sem("loaded")
        edges_in = sem("edges_in")
        filled = sem("filled")
        zeroed = sem("zeroed")
        parted = sem("parted")
        prepared = sem("prepared")
        prep_out = sem("prep_out")
        block_found = sem("block_found")
        rows_in = [sem(f"rows_in{u}") for u in range(2)]
        rows_used = sem("rows_used")
        placed = sem("placed")
        x_spread = sem("x_spread")
        ends_in = sem("ends_in")
        ends_out = sem("ends_out")
        dve_done = sem("dve_done")
        act_done = sem("act_done")
        rows_got = [[sem(f"rows_got{n}_{c}") for c in range(CHUNKS)] for n in range(2)]
        border_in = [sem(f"border_in{n}") for n in range(2)]
        centred = sem("centred")
        squared = sem("squared")
        var_ready = sem("var_ready")
        dev_ready = sem("dev_ready")
        node_ready = sem("node_ready")
        turned = sem("turned")
        turned_sb = sem("turned_sb")
        mapped = sem("mapped")
        y_ready = sem("y_ready")
        picked = sem("picked")
        added = sem("added")
        h_out = sem("h_out")
        y_out = sem("y_out")
        y_spread = sem("y_spread")
        result_out = sem("result_out")

        idx_in = [[sem(f"idx_in{n}_{u}") for u in range(2)] for n in range(2)]
        edge_in = [[sem(f"edge_in{n}_{u}") for u in range(2)] for n in range(2)]
        gathered = [[sem(f"gathered{n}_{u}") for u in range(2)] for n in range(2)]
        stored = [[sem(f"stored{n}_{u}") for u in range(2)] for n in range(2)]
        x_turned = [sem(f"x_turned{n}") for n in range(2)]
        x_ready = [sem(f"x_ready{n}") for n in range(2)]
        s_turned = [sem(f"s_turned{n}") for n in range(2)]
        d_ready = [sem(f"d_ready{n}") for n in range(2)]
        scanned = [sem(f"scanned{n}") for n in range(2)]
        o_turned = [sem(f"o_turned{n}") for n in range(2)]
        o_ready = [sem(f"o_ready{n}") for n in range(2)]
        fresh_ready = sem("fresh_ready")
        hid_done = sem("hid_done")
        relu_done = sem("relu_done")
        v_done = sem("v_done")
        onehot_ready = sem("onehot_ready")
        comp_done = sem("comp_done")
        comp_ready = sem("comp_ready")
        rel_done = sem("rel_done")
        key_done = sem("key_done")
        query_ready = sem("query_ready")
        score_ready = sem("score_ready")
        sum_done = sem("sum_done")
        weight_ready = sem("weight_ready")
        coef_done = sem("coef_done")
        prod_ready = sem("prod_ready")
        msg_done = sem("msg_done")
        wmsg_ready = sem("wmsg_ready")
        src_copied = sem("src_copied")

        waits_passed = {nc.sync: sem("sp_passed"), nc.gpsimd: sem("pool_passed")}
        N_CONST = 18
        block = ctx.enter_context(nc.Block())

        def run_steps(eng, body):
            body(0, 0)
            body(1, 1)
            with eng.Fori(1, STEPS // 2 - 1) as i:
                for u in range(2):
                    body(2 * i + u, u)
            body(STEPS - 2, 0)
            body(STEPS - 1, 1)

        def passed(eng, s):
            if not isinstance(s, int) and eng in waits_passed:
                eng.sem_inc(waits_passed[eng], 1)

        def wait_slot(eng, s, u, semaphore, each, more):
            if isinstance(s, int):
                n = (s // 2 + more) * each
                if n > 0:
                    eng.wait_ge(semaphore, n)
            else:
                eng.wait_ge(semaphore, ((s - u) // 2 + more) * each)
                passed(eng, s)

        def wait_step(eng, s, semaphore, each=1, lag=0, more=0):
            if isinstance(s, int) and (s - lag + 1) * each + more <= 0:
                return
            eng.wait_ge(semaphore, (s - lag + 1) * each + more)
            passed(eng, s)

        spread_v = spread[0:EDGES, :].rearrange("(s p k) f -> s p k f", s=STEPS, p=P)
        spread_heads = spread[0:STREAMS, :]
        max_v = max_rows.rearrange("(s p k) f -> s p k f", s=STEPS, p=P)
        sum_v = sum_rows.rearrange("(s p k) f -> s p k f", s=STEPS, p=P)
        keep_v = keep_dram.rearrange("(g s n) -> s g n", g=STREAMS, s=STEPS)
        type_v = type_dram.rearrange("(g s n) -> s g n", g=STREAMS, s=STEPS)
        ea_v = t["edge_t"].rearrange("p (s n) -> s p n", s=STEPS)
        idx_v = t["src_t"]
        h_nodes = h_dram.rearrange("(p t) (c f) -> p t c f", p=P, f=F)
        y_nodes = y_dram.rearrange("(p t) f -> p t f", p=P)
        full = N_NODES // NODE_COLS
        tail = N_NODES - full * NODE_COLS
        out_full = t["out"][0:full * NODE_COLS, :].rearrange("(p t) f -> p t f", p=full)
        out_tail = t["out"][full * NODE_COLS:, :].rearrange("(p t) f -> p t f", p=1)

        def border_rows(eng, table, n):
            ends = table[EDGES - STREAMS:EDGES, 0:F]
            eng.dma_start(border[:, :, :], ends.partition_broadcast(P)).then_inc(border_in[n], 16)

        @block.sync
        def _(sp):
            sp.dma_start(heads_i[:, :], t["heads"].partition_broadcast(P)).then_inc(edges_in, 16)
            sp.dma_start(dst_i, t["dst_rows"]).then_inc(edges_in, 16)
            sp.dma_start(prev_i, t["prev_rows"]).then_inc(edges_in, 16)
            sp.dma_start(type_i, t["type_rows"]).then_inc(edges_in, 16)
            sp.dma_start(heads4[:, :], t["heads4"]).then_inc(edges_in, 16)
            for tile, name in ((node_id, "node_id"), (spare_id, "spare_id"), (row_id, "row_id"),
                               (ident, "ident"), (w1, "w1"), (w2, "w2"), (b1, "b1"), (a1w, "a1w"),
                               (a1b, "a1b"), (a2w, "a2w"), (self_w, "self_w"), (basis, "basis"),
                               (ones_blk, "ones_blk"), (sel_f, "sel"), (x, "x_nodes")):
                full_tile = tuple(slice(None) for _ in tile.shape)
                sp.dma_start(tile[full_tile], t[name]).then_inc(loaded, 16)
            sp.dma_start(b2[:, :], t["b2"].partition_broadcast(P)).then_inc(loaded, 16)
            sp.dma_start(a2b[:, :], t["a2b"].partition_broadcast(P)).then_inc(loaded, 16)
            sp.dma_start(rel[:, :], t["rel"]).then_inc(loaded, 16)
            sp.wait_ge(prepared, 3)
            sp.dma_start(dst_blocks.rearrange("a b -> (a b)").rearrange("(p n) -> p n", p=P),
                         dst_f).then_inc(prep_out, 16)
            sp.dma_start(keep_dram.rearrange("(p n) -> p n", p=P), keep_b).then_inc(prep_out, 16)
            sp.dma_start(type_dram.rearrange("(p n) -> p n", p=P), type_b).then_inc(prep_out, 16)
            sp.wait_ge(prep_out, 48)
            sp.wait_ge(ends_in, 16)
            sp.wait_ge(x_spread, 16 * NODE_COLS)
            sp.dma_start(spread_heads, rows4[:, :]).then_inc(ends_out, 16)
            sp.wait_ge(ends_out, 16)

            def loads(n, s, u):
                wait_slot(sp, s, u, gathered[n][u], 16 * SLOTS, 0)
                sp.dma_start(src_idx[:, u, :], idx_v[s]).then_inc(idx_in[n][u], 16)
                wait_step(sp, s, s_turned[n], lag=2)
                sp.dma_start(sp_in[:, u], spread_v[s]).then_inc(edge_in[n][u], 16)
                if n == 0:
                    wait_step(sp, s, hid_done, each=2, lag=2)
                    sp.dma_start(ea[:, u, :], ea_v[s]).then_inc(edge_in[n][u], 16)
                else:
                    wait_step(sp, s, onehot_ready, lag=2)
                    sp.dma_start(types[:, u], type_v[s].partition_broadcast(P)).then_inc(edge_in[n][u], 16)
                wait_step(sp, s, scanned[n], lag=2)
                for g in range(STREAMS):
                    sp.dma_start(keep[F * g:F * g + F, u, :],
                                 keep_v[s][g].partition_broadcast(F)).then_inc(edge_in[n][u], 16)

            run_steps(sp, lambda s, u: loads(0, s, u))

            for u in range(2):
                sp.wait_ge(stored[0][u], 16 * (STEPS // 2))
            border_rows(sp, max_rows, 0)
            for c in range(CHUNKS):
                cols = slice(c * CHUNK, (c + 1) * CHUNK)
                sp.wait_ge(node_ready, c + 1)
                for k in range(4):
                    sp.dma_start(h_nodes[:, cols, k, :], h[:, cols, :]).then_inc(h_out, 16)
                sp.wait_ge(y_ready, c + 1)
                sp.dma_start(y_nodes[:, cols, :], y[:, cols, :]).then_inc(y_out, 16)
            sp.wait_ge(ends_in, 32)
            sp.wait_ge(y_spread, 16 * NODE_COLS)
            sp.dma_start(spread_heads, rows4[:, :]).then_inc(ends_out, 16)
            sp.wait_ge(ends_out, 32)

            run_steps(sp, lambda s, u: loads(1, s, u))

            for u in range(2):
                sp.wait_ge(stored[1][u], 16 * (STEPS // 2))
            border_rows(sp, sum_rows, 1)
            for c in range(CHUNKS):
                cols = slice(c * CHUNK, (c + 1) * CHUNK)
                sp.wait_ge(node_ready, CHUNKS + c + 1)
                sp.dma_start(out_full[:, cols, :], agg[0:full, cols, :]).then_inc(result_out, 16)
                got = min((c + 1) * CHUNK, tail) - c * CHUNK
                if got > 0:
                    cols = slice(c * CHUNK, c * CHUNK + got)
                    sp.dma_start(out_tail[:, cols, :], agg[full:full + 1, cols, :]).then_inc(result_out, 16)
            sp.wait_ge(result_out, 16 * (CHUNKS + -(-tail // CHUNK)))

        @block.gpsimd
        def _(pool):
            def gather(out, table, index, done):
                pool.indirect_dma_start(out=out, out_offset=None, in_=table,
                                        in_offset=bass.IndirectOffsetOnAxis(ap=index, axis=0)).then_inc(done, 16)

            def scatter(table, index, rows_, done):
                pool.indirect_dma_start(out=table, out_offset=bass.IndirectOffsetOnAxis(ap=index, axis=0),
                                        in_=rows_, in_offset=None).then_inc(done, 16)

            pool.wait_ge(edges_in, 80)
            gather(rows4[:, :], t["x_dram"], heads4[:, :], ends_in)
            pool.wait_ge(prep_out, 48)
            for c in range(SEARCHES):
                pool.wait_ge(block_found, c + 1)
                if c >= 2:
                    pool.wait_ge(rows_used, c - 1)
                for k in range(c * SEARCH, min((c + 1) * SEARCH, NODE_COLS + 1)):
                    gather(rows[:, c % 2, k - c * SEARCH, :], dst_blocks, block_i[:, k:k + 1], rows_in[c % 2])
            pool.wait_ge(placed, 1)
            pool.wait_ge(loaded, 16 * N_CONST)
            pool.wait_ge(zeroed, 16 * N_ZERO)
            for k in range(NODE_COLS):
                scatter(spread, place_i[:, k:k + 1], x[:, k, :], x_spread)

            def gathers(n, s, u):
                wait_slot(pool, s, u, idx_in[n][u], 16, 1)
                wait_step(pool, s, x_turned[n], lag=2)
                if n == 1:
                    wait_step(pool, s, src_copied, lag=2)
                for k in range(SLOTS):
                    gather((xg0, xg)[n][:, u, k, :], (t["x_dram"], h_dram)[n], src_idx[:, u, k:k + 1], gathered[n][u])

            run_steps(pool, lambda s, u: gathers(0, s, u))

            for u in range(2):
                pool.wait_ge(stored[0][u], 16 * (STEPS // 2))
            for c in range(CHUNKS):
                for k in range(c * CHUNK, (c + 1) * CHUNK):
                    gather(agg[:, k, :], max_rows, last_i[:, k:k + 1], rows_got[0][c])
            pool.wait_ge(ends_out, 16)
            for c in range(CHUNKS):
                pool.wait_ge(y_ready, c + 1)
                for k in range(c * CHUNK, (c + 1) * CHUNK):
                    scatter(spread, place_i[:, k:k + 1], y[:, k, :], y_spread)
            pool.wait_ge(y_out, 16 * CHUNKS)
            gather(rows4[:, :], y_dram, heads4[:, :], ends_in)
            pool.wait_ge(h_out, 4 * 16 * CHUNKS)

            run_steps(pool, lambda s, u: gathers(1, s, u))

            for u in range(2):
                pool.wait_ge(stored[1][u], 16 * (STEPS // 2))
            for c in range(CHUNKS):
                if c >= 2:
                    pool.wait_ge(added, c - 1)
                    pool.wait_ge(picked, c - 1)
                for k in range(CHUNK):
                    col = c * CHUNK + k
                    gather(last_rows[:, c % 2, k, :], sum_rows, last_i[:, col:col + 1], rows_got[1][c])

        @block.scalar
        def _(act):
            act.wait_ge(filled, 3)
            flat = spread[0:EDGES, :].rearrange("e f -> (e f)")
            for k in range(N_ZERO):
                n = min(ZERO, EDGES * F // P - k * ZERO)
                act.dma_start(flat[k * P * ZERO:k * P * ZERO + P * n].rearrange("(p n) -> p n", p=P),
                              zero[:, 0:n]).then_inc(zeroed, 16)
            act.wait_ge(loaded, 16 * N_CONST)

            def store(n, s, u, tile, view):
                wait_step(act, s, o_ready[n])
                act.dma_start(view[s], tile).then_inc(stored[n][u], 16)

            def step0(s, u):
                wait_step(act, s, x_turned[0])
                wait_step(act, s, hid_done, each=2, lag=2)
                act.copy(xt[:, u, :], bank[0][:, :]).then_inc(x_ready[0], 1)
                for q in range(2):
                    wait_step(act, s, hid_done, each=2, more=q - 1)
                    wait_step(act, s, v_done, lag=2)
                    act.activation(hid[:, u, q, :], bank[2 + q][:, :], ACT.Relu,
                                   bias=b1[:, 0:1]).then_inc(relu_done, 1)
                wait_step(act, s, o_turned[0])
                wait_slot(act, s, u, stored[0][u], 16, 0)
                act.copy(out0[:, u].rearrange("p k f -> p (k f)"), bank[5][:, :]).then_inc(o_ready[0], 1)
                store(0, s, u, out0[:, u], max_v)

            run_steps(act, step0)

            def layer_norm(n):
                act.wait_ge(centred, n + 1)
                act.activation(node_c[:, :, :], node_b[:, :, :], ACT.Square).then_inc(squared, 1)
                act.wait_ge(var_ready, n + 1)
                act.activation(stat_b[:, :], stat_a[:, :], ACT.Sqrt, bias=eps[:, 0:1],
                               scale=1.0 / F).then_inc(dev_ready, 1)

            def turned_copy(n):
                act.wait_ge(turned, n + 1)
                if n > 0:
                    act.wait_ge(mapped, n)
                whole = P * sum(b - a == 4 for a, b in GROUPS)
                rest_rows = F * (CHUNK % 4)
                act.copy(node_t[:, 0:whole], bank[6][:, 0:whole])
                act.copy(node_t[0:rest_rows, whole:whole + P],
                         bank[6][0:rest_rows, whole:whole + P]).then_inc(turned_sb, 1)

            for c in range(CHUNKS):
                layer_norm(c)
                turned_copy(c)

            def step1(s, u):
                for q in range(2):
                    wait_step(act, s, comp_done)
                    wait_step(act, s, prod_ready, each=SLOTS, lag=1)
                    act.copy(comp[:, q, :], bank[2 + q][:, :]).then_inc(comp_ready, 1)
                for g in range(STREAMS):
                    wait_step(act, s, x_turned[1], each=STREAMS, more=g - 3)
                    wait_step(act, s, prod_ready, each=SLOTS, lag=2)
                    wait_step(act, s, key_done, lag=2)
                    act.copy(x4[:, u, g, :], bank[g % 2][:, :]).then_inc(x_ready[1], 1)
                wait_slot(act, s, u, gathered[1][u], 16 * SLOTS, 1)
                wait_slot(act, s, u, stored[1][u], 16, 0)
                act.copy(out1[:, u, :, F:2 * F], xg[:, u, :, 0:F]).then_inc(src_copied, 1)
                if not isinstance(s, int) or s >= 1:
                    finish1(s - 1, 1 - u)
                wait_step(act, s, sum_done)
                wait_step(act, s, wmsg_ready, lag=1)
                act.activation(weight, bank[1][:, :], ACT.Tanh, scale=float(F) ** -0.5
                               ).then_inc(weight_ready, 1)

            def finish1(s, u):
                wait_step(act, s, o_turned[1])
                act.copy(out1[:, u, :, 0:F], bank[4][:, :].rearrange("p (k f) -> p k f", f=F)).then_inc(o_ready[1], 1)
                wait_step(act, s, src_copied)
                store(1, s, u, out1[:, u], sum_v)

            run_steps(act, step1)
            finish1(STEPS - 1, 1)

            for c in range(CHUNKS):
                act.wait_ge(rows_got[1][c], 16 * CHUNK)
                if c > 0:
                    act.wait_ge(turned, CHUNKS + c)
                act.copy(y[:, 0:CHUNK, :], last_rows[:, c % 2, :, F:2 * F]).then_inc(picked, 1)
                turned_copy(CHUNKS + c)
                layer_norm(CHUNKS + c)

        @block.vector
        def _(dve):
            done = [0]

            def link(ins):
                done[0] += 1
                ins.then_inc(dve_done, 1)
                dve.wait_ge(dve_done, done[0])

            dve.memset(zero, 0.0).then_inc(filled, 1)
            dve.memset(eps[:, :], EPS).then_inc(filled, 1)
            dve.memset(rest[:, :], 0.0).then_inc(filled, 1)
            dve.memset(comp_lhs[:, :], 0.0).then_inc(filled, 1)
            dve.wait_ge(edges_in, 80)
            dve.tensor_copy(dst_f, dst_i).then_inc(prepared, 1)
            dve.tensor_tensor(keep_b, dst_i, prev_i, ALU.is_equal).then_inc(prepared, 1)
            dve.tensor_copy(type_b, type_i).then_inc(prepared, 1)
            link(dve.tensor_copy(heads[:, :], heads_i[:, :]))

            dve.wait_ge(loaded, 16 * N_CONST)

            def count(values, node, total):
                link(dve.tensor_scalar(below[:, 0, 0:values.shape[-1]], values, node_id[:, node:node + 1], None,
                                       ALU.is_lt, ALU.add, accum_out=total[:, node:node + 1]))

            def find_blocks(c):
                cols = slice(c * SEARCH, min((c + 1) * SEARCH, NODE_COLS + 1))
                for k in range(cols.start, cols.stop):
                    count(heads[:, :], k, block_f)
                link(dve.tensor_scalar(block_f[:, cols], block_f[:, cols], -1.0, 0.0, ALU.add, ALU.max))
                dve.tensor_copy(block_i[:, cols], block_f[:, cols]).then_inc(block_found, 1)

            def find_edges(c):
                cols = slice(c * SEARCH, min((c + 1) * SEARCH, NODE_COLS + 1))
                got = sum(len(range(d * SEARCH, min((d + 1) * SEARCH, NODE_COLS + 1)))
                          for d in range(c % 2, c + 1, 2))
                dve.wait_ge(rows_in[c % 2], 16 * got)
                for k in range(cols.start, cols.stop):
                    count(rows[:, c % 2, k - cols.start, :], k, inside)
                dve.scalar_tensor_tensor(first[:, cols], block_f[:, cols], float(BLOCK), inside[:, cols],
                                         ALU.mult, ALU.add).then_inc(rows_used, 1)

            find_blocks(0)
            for c in range(SEARCHES):
                if c + 1 < SEARCHES:
                    find_blocks(c + 1)
                find_edges(c)
            dve.wait_ge(rows_used, SEARCHES)
            begin, end = first[:, 0:NODE_COLS], first[:, 1:NODE_COLS + 1]
            link(dve.tensor_tensor(has[:, :], end, begin, ALU.is_gt))
            link(dve.tensor_scalar(last[:, :], end, -1.0, 0.0, ALU.add, ALU.max))

            def table_row(edge, out):
                link(dve.tensor_scalar(out, edge, float(STREAMS), None, ALU.mult))
                for g in range(1, STREAMS):
                    link(dve.tensor_scalar(past[:, :], edge, float(g * STREAM), float(1 - EDGES), ALU.is_ge,
                                           ALU.mult))
                    link(dve.tensor_tensor(out, out, past[:, :], ALU.add))

            table_row(last[:, :], place[:, :])
            link(dve.tensor_copy(last_i[:, :], place[:, :]))
            table_row(begin, place[:, :])
            link(dve.tensor_tensor(place[:, :], place[:, :], spare_id[:, :], ALU.subtract))
            link(dve.tensor_tensor(place[:, :], place[:, :], has[:, :], ALU.mult))
            link(dve.tensor_tensor(place[:, :], place[:, :], spare_id[:, :], ALU.add))
            dve.tensor_copy(place_i[:, :], place[:, :]).then_inc(placed, 1)
            link(dve.tensor_scalar(no_edge[:, :], has[:, :], -1.0, BIG, ALU.add, ALU.mult))
            for g in range(1, STREAMS):
                link(dve.tensor_scalar(crosses2[:, g, :], begin, float(g * STREAM), None, ALU.is_lt))
                link(dve.tensor_scalar(crosses[:, g, :], last[:, :], float(g * STREAM), None, ALU.is_ge))
                link(dve.tensor_tensor(crosses[:, g, :], crosses[:, g, :], crosses2[:, g, :], ALU.mult))
                link(dve.tensor_scalar(no_cross[:, g, :], crosses[:, g, :], -1.0, BIG, ALU.add, ALU.mult))

            link(dve.tensor_copy(rel_parts[:, 0, :], rel[:, :]))
            link(dve.tensor_tensor(rest[:, :], rel[:, :], rel_parts[:, 0, :], ALU.subtract))
            link(dve.tensor_copy(rel_parts[:, 1, :], rest[:, :]))
            link(dve.tensor_tensor(rest2[:, :], rest[:, :], rel_parts[:, 1, :], ALU.subtract))
            link(dve.tensor_copy(rel_parts[:, 2, :], rest2[:, :]))
            for q in range(PARTS):
                link(dve.tensor_copy(comp_lhs[:, q * BASES:(q + 1) * BASES], rel_parts[:, q, F:F + BASES]))
            dve.tensor_copy(sel[:, :, :], sel_f[:, :, :]).then_inc(parted, 1)

            def before(s, u, tile):
                return 0.0 if isinstance(s, int) and s == 0 else tile[:, 1 - u, LEN - 1:LEN]

            def step0(s, u):
                wait_slot(dve, s, u, edge_in[0][u], 16 * 6, 1)
                wait_step(dve, s, scanned[0], lag=2)
                dve.tensor_scalar(fresh[:, u, :], keep[:, u, :], -1.0, BIG, ALU.add, ALU.mult
                                  ).then_inc(fresh_ready, 1)
                wait_step(dve, s, s_turned[0])
                wait_step(dve, s, hid_done, each=2, lag=2)
                wait_step(dve, s, d_ready[0], lag=1)
                dve.tensor_tensor_scan(dt_[:, u, :], keep[:, u, :], bank[1][:, :], before(s, u, dt_),
                                       ALU.mult, ALU.add).then_inc(d_ready[0], 1)
                wait_step(dve, s, v_done)
                wait_step(dve, s, fresh_ready)
                wait_step(dve, s, o_turned[0], lag=2)
                wait_step(dve, s, scanned[0], lag=1)
                dve.tensor_tensor_scan(scan[:, u, :], fresh[:, u, :], bank[4][:, :],
                                       -BIG if isinstance(s, int) and s == 0 else before(s, u, scan),
                                       ALU.add, ALU.max).then_inc(scanned[0], 1)

            run_steps(dve, step0)

            shape = [P, CHUNK, F]

            def layer_norm(n, out):
                link(dve.tensor_reduce(stat_a[:, :], node_a[:, :, :], AX.X, ALU.add))
                link(dve.tensor_scalar(stat_c[:, :], stat_a[:, :], 1.0 / F, None, ALU.mult))
                dve.tensor_tensor(node_b[:, :, :], node_a[:, :, :], bc(stat_c[:, :], shape, 2), ALU.subtract
                                  ).then_inc(centred, 1)
                dve.wait_ge(centred, n + 1)
                dve.wait_ge(squared, n + 1)
                dve.tensor_reduce(stat_a[:, :], node_c[:, :, :], AX.X, ALU.add).then_inc(var_ready, 1)
                dve.wait_ge(dev_ready, n + 1)
                link(dve.reciprocal(stat_c[:, :], stat_b[:, :]))
                dve.tensor_tensor(out, node_b[:, :, :], bc(stat_c[:, :], shape, 2), ALU.mult
                                  ).then_inc(node_ready, 1)
                dve.wait_ge(node_ready, n + 1)

            dve.wait_ge(border_in[0], 16)
            for c in range(CHUNKS):
                cols = slice(c * CHUNK, (c + 1) * CHUNK)
                dve.wait_ge(rows_got[0][c], 16 * CHUNK)
                v = agg[:, cols, :]
                for g in range(1, STREAMS):
                    link(dve.tensor_tensor(node_b[:, :, :], bc(border[:, g - 1, :], shape, 1),
                                           bc(no_cross[:, g, cols], shape, 2), ALU.add))
                    link(dve.tensor_tensor(v, v, node_b[:, :, :], ALU.max))
                link(dve.tensor_tensor(v, v, bc(b2[:, :], shape, 1), ALU.add))
                link(dve.tensor_tensor(v, v, bc(no_edge[:, cols], shape, 2), ALU.add))
                link(dve.tensor_tensor(v, v, x[:, cols, :], ALU.max))
                link(dve.tensor_tensor(node_a[:, :, :], v, x[:, cols, :], ALU.add))
                layer_norm(c, h[:, cols, :])
                dve.wait_ge(mapped, c + 1)
                dve.tensor_tensor(y[:, cols, :], bank[7][:, 0:CHUNK * F].rearrange("p (t f) -> p t f", f=F),
                                  bc(a2b[:, :], shape, 1), ALU.add).then_inc(y_ready, 1)

            def one_hot(s, u):
                wait_slot(dve, s, u, edge_in[1][u], 16 * 6, 1)
                wait_step(dve, s, rel_done, lag=2)
                dve.tensor_scalar(onehot[:, u, :, :], types[:, u, :, :], row_id[:, 0:1], None, ALU.is_equal
                                  ).then_inc(onehot_ready, 1)

            def step1(s, u):
                wait_step(dve, s, s_turned[1])
                wait_step(dve, s, d_ready[1], lag=1)
                wait_step(dve, s, query_ready, lag=2)
                wait_slot(dve, s, u, edge_in[1][u], 16 * 6, 1)
                dve.tensor_tensor_scan(dt_[:, u, :], keep[:, u, :], bank[4][:, :], before(s, u, dt_),
                                       ALU.mult, ALU.add).then_inc(d_ready[1], 1)
                wait_step(dve, s, d_ready[1])
                wait_step(dve, s, rel_done)
                wait_step(dve, s, score_ready, lag=1)
                dve.tensor_tensor(query, dt_[:, u, :], bank[5][:, :], ALU.add).then_inc(query_ready, 1)
                wait_step(dve, s, query_ready)
                wait_step(dve, s, key_done)
                wait_step(dve, s, sum_done, lag=1)
                dve.scalar_tensor_tensor(score, bank[0][:, :], a1b[:, 0:1], query,
                                         ALU.add, ALU.mult).then_inc(score_ready, 1)
                for k in range(KCH):
                    for g in range(STREAMS):
                        n = k * STREAMS + g
                        wait_step(dve, s, coef_done, each=SLOTS, more=n - SLOTS + 1)
                        wait_step(dve, s, x_ready[1], each=STREAMS, more=g - 3)
                        wait_step(dve, s, msg_done, each=KCH, more=k - 3 - G_BUFS // STREAMS)
                        dve.tensor_tensor(prod[:, n % G_BUFS, :], x4[:, u, g, :],
                                          bank[(2, 3, 6)[n % C_BANKS]][:, :], ALU.mult).then_inc(prod_ready, 1)
                    if k == 1 and (not isinstance(s, int) or s + 1 < STEPS):
                        one_hot(s + 1, 1 - u)
                wait_step(dve, s, msg_done, each=KCH)
                wait_step(dve, s, weight_ready)
                wait_step(dve, s, scanned[1], lag=1)
                dve.scalar_tensor_tensor(wmsg, weight, 0.0, bank[7][:, :], ALU.max, ALU.mult
                                         ).then_inc(wmsg_ready, 1)
                wait_step(dve, s, wmsg_ready)
                wait_step(dve, s, o_turned[1], lag=2)
                dve.tensor_tensor_scan(scan[:, u, :], keep[:, u, :], wmsg, before(s, u, scan),
                                       ALU.mult, ALU.add).then_inc(scanned[1], 1)

            one_hot(0, 0)
            run_steps(dve, step1)

            dve.wait_ge(border_in[1], 16)
            for c in range(CHUNKS):
                cols = slice(c * CHUNK, (c + 1) * CHUNK)
                dve.wait_ge(rows_got[1][c], 16 * CHUNK)
                v = agg[:, cols, :]
                nei = last_rows[:, c % 2, :, 0:F]
                for g in range(1, STREAMS):
                    link(dve.tensor_tensor(node_b[:, :, :], bc(border[:, g - 1, :], shape, 1),
                                           bc(crosses[:, g, cols], shape, 2), ALU.mult))
                    link(dve.tensor_tensor(v, nei if g == 1 else v, node_b[:, :, :], ALU.add))
                dve.wait_ge(mapped, CHUNKS + c + 1)
                dve.tensor_tensor(node_a[:, :, :], v, bank[7][:, 0:CHUNK * F].rearrange("p (t f) -> p t f", f=F),
                                  ALU.add).then_inc(added, 1)
                dve.wait_ge(added, c + 1)
                link(dve.tensor_tensor(node_b[:, :, :], node_a[:, :, :], bc(has[:, cols], shape, 2), ALU.mult))
                link(dve.scalar_tensor_tensor(node_a[:, :, :], node_b[:, :, :], 0.0, h[:, cols, :],
                                              ALU.max, ALU.add))
                layer_norm(CHUNKS + c, v)

        @block.tensor
        def _(pe):
            pe.wait_ge(loaded, 16 * N_CONST)
            pe.wait_ge(parted, 1)

            def spread_turn(n, s, u, b):
                wait_slot(pe, s, u, edge_in[n][u], 16 * 6, 1)
                out = bank[b][:, :].rearrange("p (n j) -> p j n", j=TILES)
                for j in range(TILES):
                    last_ = pe.transpose(out[:, j, :], sp_in[:, u, j * STREAMS:(j + 1) * STREAMS, :], ident[:, :])
                last_.then_inc(s_turned[n], 1)

            def scan_turn(n, s, u, b):
                wait_step(pe, s, scanned[n])
                src = scan[:, u, :].rearrange("p (n j) -> p j n", j=TILES)
                for j in range(TILES):
                    last_ = pe.transpose(bank[b][:, P * j:P * j + P], src[:, j, :], ident[:, :])
                last_.then_inc(o_turned[n], 1)

            def step0(s, u):
                wait_slot(pe, s, u, gathered[0][u], 16 * SLOTS, 1)
                wait_step(pe, s, x_ready[0], lag=1)
                out = bank[0][:, :].rearrange("p (n j) -> p j n", j=TILES)
                for j in range(TILES):
                    last_ = pe.transpose(out[:, j, :], xg0[:, u, j * STREAMS:(j + 1) * STREAMS, :], ident[:, :])
                last_.then_inc(x_turned[0], 1)
                wait_step(pe, s, d_ready[0], lag=1)
                spread_turn(0, s, u, 1)
                wait_step(pe, s, x_ready[0])
                wait_step(pe, s, d_ready[0])
                for q in range(2):
                    wait_step(pe, s, relu_done, each=2, lag=1, more=q - 1)
                    for k, rhs in enumerate((xt, ea, dt_)):
                        last_ = pe.matmul(bank[2 + q][:, :], w1[:, (0, 2, 1)[k], q, :], rhs[:, u, :],
                                          start=k == 0, stop=k == 2)
                    last_.then_inc(hid_done, 1)
                wait_step(pe, s, scanned[0], lag=1)
                for q in range(2):
                    wait_step(pe, s, relu_done, each=2, more=q - 1)
                    last_ = pe.matmul(bank[4][:, :], w2[:, q, :], hid[:, u, q, :], start=q == 0, stop=q == 1)
                last_.then_inc(v_done, 1)
                wait_step(pe, s, o_ready[0], lag=1)
                scan_turn(0, s, u, 5)

            run_steps(pe, step0)

            def node_map(n, source, weights):
                if n > 0:
                    pe.wait_ge(turned_sb, n)
                for k, (a, b) in enumerate(GROUPS):
                    m = F * (b - a)
                    last_ = pe.transpose(bank[6][0:m, P * k:P * k + P], source[:, a:b, :], ident[:, :])
                last_.then_inc(turned, 1)
                pe.wait_ge(turned_sb, n + 1)
                for k, (a, b) in enumerate(GROUPS):
                    m = F * (b - a)
                    last_ = pe.matmul(bank[7][:, F * a:F * b], node_t[0:m, P * k:P * k + P],
                                      weights[0:m, 0:m], start=True, stop=True)
                last_.then_inc(mapped, 1)

            for c in range(CHUNKS):
                pe.wait_ge(node_ready, c + 1)
                if c > 0:
                    pe.wait_ge(y_ready, c)
                node_map(c, h[:, c * CHUNK:(c + 1) * CHUNK, :], a2w)

            def coefs(s, u, k):
                for g in range(STREAMS):
                    n = k * STREAMS + g
                    wait_step(pe, s, prod_ready, each=SLOTS, more=n - C_BANKS + 1 - SLOTS)
                    pe.matmul(bank[(2, 3, 6)[n % C_BANKS]][:, :], sel[:, (g % 2) * KCH + k, :], comp[:, g // 2, :],
                              start=True, stop=True).then_inc(coef_done, 1)

            def messages(s, u, k):
                wait_step(pe, s, prod_ready, each=SLOTS, more=(k + 1) * STREAMS - SLOTS)
                for g in range(STREAMS):
                    last_ = pe.matmul(bank[7][F * g:F * g + F, :], basis[:, k, :],
                                      prod[:, (k * STREAMS + g) % G_BUFS, :], start=k == 0, stop=k == KCH - 1,
                                      tile_position=(0, F * g))
                last_.then_inc(msg_done, 1)

            def step1(s, u):
                wait_step(pe, s, onehot_ready)
                wait_step(pe, s, prod_ready, each=SLOTS, lag=1)
                for g in range(STREAMS):
                    o = 64 * (g % 2)
                    last_ = pe.matmul(bank[2 + g // 2][o:o + 64, :], comp_lhs[:, :], onehot[:, u, g, :],
                                      start=True, stop=True, tile_position=(0, o))
                last_.then_inc(comp_done, 1)
                wait_step(pe, s, query_ready, lag=1)
                for q in range(PARTS):
                    for g in range(STREAMS):
                        last_ = pe.matmul(bank[5][F * g:F * g + F, :], rel_parts[:, q, 0:F], onehot[:, u, g, :],
                                          start=q == 0, stop=q == PARTS - 1, tile_position=(0, F * g))
                last_.then_inc(rel_done, 1)
                wait_step(pe, s, o_ready[1], lag=2)
                spread_turn(1, s, u, 4)
                wait_slot(pe, s, u, gathered[1][u], 16 * SLOTS, 1)
                for g in range(STREAMS):
                    if g == 0:
                        wait_step(pe, s, score_ready, lag=1)
                    elif g == 1:
                        wait_step(pe, s, weight_ready, lag=1)
                    else:
                        wait_step(pe, s, x_ready[1], each=STREAMS, more=g - 2 - 3)
                    out = bank[g % 2][:, :].rearrange("p (n j) -> p j n", j=TILES)
                    for j in range(TILES):
                        last_ = pe.transpose(out[:, j, :], xg[:, u, j * STREAMS + g, :],
                                             ident[:, :])
                    last_.then_inc(x_turned[1], 1)
                wait_step(pe, s, x_ready[1], each=STREAMS)
                for g in range(STREAMS):
                    last_ = pe.matmul(bank[0][F * g:F * g + F, :], a1w[:, :], x4[:, u, g, :],
                                      start=True, stop=True, tile_position=(0, F * g))
                last_.then_inc(key_done, 1)
                if not isinstance(s, int) or s >= 1:
                    wait_step(pe, s, d_ready[1])
                    scan_turn(1, s - 1, 1 - u, 4)
                wait_step(pe, s, comp_ready, each=2)
                coefs(s, u, 0)
                coefs(s, u, 1)
                wait_step(pe, s, wmsg_ready, lag=1)
                messages(s, u, 0)
                wait_step(pe, s, score_ready)
                pe.matmul(bank[1][:, :], ones_blk[:, :], score, start=True, stop=True).then_inc(sum_done, 1)
                coefs(s, u, 2)
                messages(s, u, 1)
                coefs(s, u, 3)
                messages(s, u, 2)
                messages(s, u, 3)

            run_steps(pe, step1)
            scan_turn(1, STEPS - 1, 1, 4)

            for c in range(CHUNKS):
                pe.wait_ge(picked, c + 1)
                if c > 0:
                    pe.wait_ge(added, c)
                node_map(CHUNKS + c, y[:, 0:CHUNK, :], self_w)


N_ZERO = -(-(EDGES * F) // (P * 4096))


def _blocks(a, n):
    r, c = a.shape
    out = np.zeros((n * r, n * c), a.dtype)
    for i in range(n):
        out[i * r:(i + 1) * r, i * c:(i + 1) * c] = a
    return out


def kernel(x, src, dst, edge_attr_32, edge_type_86, L0_gnn_W1, L0_gnn_b1, L0_gnn_W2, L0_gnn_b2,
           L1_gnn_weight, L1_gnn_w_comp, L1_gnn_self_loop_weight, L1_gnn_A1_w, L1_gnn_A1_b,
           L1_gnn_A2_w, L1_gnn_A2_b, L1_gnn_rel_emb):
    from concourse import bacc
    from concourse.bass_utils import run_bass_kernel_spmd

    f32 = np.float32
    xs, src, dst, types, attr = (np.asarray(a) for a in (x, src, dst, edge_type_86, edge_attr_32))
    pad = EDGES - N_EDGES
    x_pad = np.concatenate([xs, np.zeros((NODES - N_NODES, F), f32)])
    src_pad = np.concatenate([src, np.zeros(pad, src.dtype)])
    dst_pad = np.concatenate([dst, np.full(pad, NODES, dst.dtype)])
    type_pad = np.concatenate([types, np.zeros(pad, types.dtype)])
    attr_pad = np.concatenate([attr, np.zeros((pad, F), f32)])
    prev = np.concatenate([np.full(1, -1, dst.dtype), dst_pad[:-1]])

    W1 = np.asarray(L0_gnn_W1).reshape(3, F, HID)
    w1 = np.zeros((P, 3, 2, P), f32)
    w2 = np.zeros((P, 2, P), f32)
    for g in range(STREAMS):
        q, o = g // 2, HID * (g % 2)
        w1[F * g:F * g + F, :, q, o:o + HID] = W1.transpose(1, 0, 2)
        w2[o:o + HID, q, F * g:F * g + F] = np.asarray(L0_gnn_W2)
    sel = np.zeros((2, 64, 2, KCH, 4, F), f32)
    for half in range(2):
        for q in range(PARTS):
            for k in range(KCH):
                for b in range(4):
                    sel[half, q * BASES + 4 * k + b, half, k, b, :] = 1.0
    rel = np.zeros((P, F + BASES), f32)
    n_types = np.asarray(L1_gnn_rel_emb).shape[0]
    rel[:n_types, :F] = np.asarray(L1_gnn_rel_emb)
    rel[:n_types, F:] = np.asarray(L1_gnn_w_comp)
    nodes = (np.arange(P)[:, None] * NODE_COLS + np.arange(NODE_COLS + 1)[None, :]).astype(f32)

    arrays = {
        "x_dram": x_pad,
        "x_nodes": x_pad.reshape(P, NODE_COLS, F),
        "src_t": src_pad.reshape(STREAMS, STEPS, P, TILES).transpose(1, 2, 3, 0).reshape(STEPS, P, SLOTS),
        "dst_rows": dst_pad.reshape(P, ROW),
        "prev_rows": prev.reshape(P, ROW),
        "type_rows": type_pad.reshape(P, ROW),
        "heads": dst_pad[::BLOCK],
        "heads4": dst_pad[::STREAM].reshape(STREAMS, 1),
        "edge_t": attr_pad.reshape(STREAMS, STREAM, F).transpose(0, 2, 1).reshape(P, STREAM),
        "w1": w1,
        "w2": w2,
        "b1": np.tile(np.asarray(L0_gnn_b1), 2).reshape(P, 1),
        "b2": np.asarray(L0_gnn_b2),
        "a1w": np.concatenate([np.asarray(L1_gnn_A1_w).T, np.zeros((P - F, F), f32)]),
        "a1b": np.tile(np.asarray(L1_gnn_A1_b), 4).reshape(P, 1),
        "a2w": _blocks(np.asarray(L1_gnn_A2_w).T, 4),
        "a2b": np.asarray(L1_gnn_A2_b),
        "self_w": _blocks(np.asarray(L1_gnn_self_loop_weight), 4),
        "basis": np.asarray(L1_gnn_weight).reshape(KCH, P, F).transpose(1, 0, 2),
        "rel": rel,
        "ident": np.eye(P, dtype=f32),
        "ones_blk": _blocks(np.ones((F, F), f32), 4),
        "sel": sel.reshape(P, 2 * KCH, P),
        "row_id": np.arange(P, dtype=f32).reshape(P, 1),
        "node_id": nodes,
        "spare_id": nodes[:, :NODE_COLS] + EDGES,
    }
    arrays = {k: np.ascontiguousarray(a) for k, a in arrays.items()}

    nc = bacc.Bacc("TRN2", target_bir_lowering=False, num_devices=1)
    t = {k: nc.dram_tensor("in_" + k, a.shape, mybir.dt.from_np(a.dtype), kind="ExternalInput").ap()
         for k, a in arrays.items()}
    t["out"] = nc.dram_tensor("out", (N_NODES, F), fp32, kind="ExternalOutput").ap()
    build(nc, t)
    r = run_bass_kernel_spmd(nc, [{"in_" + k: a for k, a in arrays.items()}], core_ids=[0])
    return r.results[0]["out"]
```

```python
from contextlib import ExitStack

import numpy as np

import concourse.bass as bass
from concourse import mybir

P = 128
N_NODES, N_EDGES = 12500, 212500
F = 32
HID = 64
BASES = 16
STREAMS = 4
LEN = 512
TILES = LEN // P
SLOTS = STREAMS * TILES
STEPS = -(-N_EDGES // (STREAMS * LEN))
STEPS += -STEPS % 8
STREAM = STEPS * LEN
EDGES = STREAMS * STREAM
ROW = EDGES // P
NODE_COLS = -(-N_NODES // P)
NODES = P * NODE_COLS
CHUNK = 14
CHUNKS = NODE_COLS // CHUNK
GROUPS = [(a, min(a + 4, CHUNK)) for a in range(0, CHUNK, 4)]
BLOCK = 512
BLOCKS = EDGES // BLOCK
SEARCH = 10
SEARCHES = -(-(NODE_COLS + 1) // SEARCH)
PARTS = 3
KCH = BASES // 4
BIG = 3.0e38
EPS = 1e-5
PRE = 8
C_BANK = [(2, 3, 6)[n % 3] for n in range(SLOTS - 1)] + [3]
C_FREE = [max(m for m in range(-SLOTS, n) if C_BANK[m % SLOTS] == C_BANK[n]) + 1 for n in range(SLOTS)]
G_BUFS = 8

fp32, bf16, i32 = mybir.dt.float32, mybir.dt.bfloat16, mybir.dt.int32
ALU = mybir.AluOpType
ACT = mybir.ActivationFunctionType
AX = mybir.AxisListType


def bc(ap, shape, axis):
    return ap.unsqueeze(axis).broadcast_to(shape)


class Step:

    def __init__(self, unroll, i, off):
        self.unroll, self.i, self.off = unroll, i, off
        self.known = isinstance(i, int)
        self.at = i * unroll + off

    def plus(self, n):
        return Step(self.unroll, self.i, self.off + n)

    def slot(self, n):
        return self.off % n

    def earlier(self, n):
        return self.i * (self.unroll // n) + self.off // n

    def exists(self):
        return not self.known or 0 <= self.at < STEPS


def run_steps(eng, body, unroll):
    for off in range(unroll):
        body(Step(unroll, 0, off))
    with eng.Fori(1, STEPS // unroll - 1) as i:
        for off in range(unroll):
            body(Step(unroll, i, off))
    for off in range(unroll):
        body(Step(unroll, STEPS // unroll - 1, off))


def build(nc, t):
    ctx = ExitStack()
    with ctx:
        def sb(name, shape, dt=fp32):
            return ctx.enter_context(nc.sbuf_tensor(name, shape, dt))

        def dram(name, shape, dt=fp32):
            return nc.dram_tensor(name, shape, dt, kind="Internal").ap()

        def sem(name):
            return ctx.enter_context(nc.semaphore(name))

        dst_blocks = dram("dst_blocks", [BLOCKS, BLOCK])
        keep_dram = dram("keep_dram", [EDGES], bf16)
        type_dram = dram("type_dram", [EDGES], bf16)
        spread = dram("spread", [EDGES + NODES, F])
        max_rows = dram("max_rows", [EDGES, F])
        sum_rows = dram("sum_rows", [EDGES, 2 * F])
        h_dram = dram("h_dram", [NODES, 4 * F])
        y_dram = dram("y_dram", [NODES, F])

        ident = sb("ident", [P, P])
        w1 = sb("w1", [P, 3, 2, P])
        w2 = sb("w2", [P, 2, P])
        b1 = sb("b1", [P, 1])
        b2 = sb("b2", [P, F])
        a1w = sb("a1w", [P, F])
        a1b = sb("a1b", [P, 1])
        a2w = sb("a2w", [P, P])
        a2b = sb("a2b", [P, F])
        self_w = sb("self_w", [P, P])
        basis = sb("basis", [P, KCH, F])
        ones_blk = sb("ones_blk", [P, P])
        sel = sb("sel", [P, 2 * KCH, P], bf16)
        rel = sb("rel", [P, F + BASES])
        rest = sb("rest", [P, F + BASES])
        rest2 = sb("rest2", [P, F + BASES])
        rel_parts = sb("rel_parts", [P, PARTS, F + BASES], bf16)
        comp_lhs = sb("comp_lhs", [P, 64], bf16)
        row_id = sb("row_id", [P, 1])
        node_id = sb("node_id", [P, NODE_COLS + 1])
        node_half = sb("node_half", [P, NODE_COLS + 1])
        spare_id = sb("spare_id", [P, NODE_COLS])
        eps = sb("eps", [P, 1])

        x = sb("x", [P, NODE_COLS, F])
        early = sb("early", [P, 3 * NODE_COLS * F])
        h = early[:, 0:NODE_COLS * F].rearrange("p (t f) -> p t f", f=F)
        y = early[:, NODE_COLS * F:2 * NODE_COLS * F].rearrange("p (t f) -> p t f", f=F)
        agg = early[:, 2 * NODE_COLS * F:].rearrange("p (t f) -> p t f", f=F)
        dst_i = early[:, 0:ROW].bitcast(i32)
        prev_i = early[:, ROW:2 * ROW].bitcast(i32)
        type_i = early[:, 2 * ROW:3 * ROW].bitcast(i32)
        dst_f = early[:, 3 * ROW:4 * ROW]
        keep_b = early[:, 4 * ROW:4 * ROW + ROW // 2].bitcast(bf16)
        type_b = early[:, 4 * ROW + ROW // 2:5 * ROW].bitcast(bf16)
        sel_f = early[:, 5 * ROW:5 * ROW + 2 * KCH * P].rearrange("p (k n) -> p k n", n=P)
        heads_i = sb("heads_i", [P, BLOCKS], i32)
        heads = sb("heads", [P, BLOCKS])
        below = sb("below", [P, BLOCK], bf16)
        signs = sb("signs", [P, BLOCK], bf16)
        side = sb("side", [P, NODE_COLS + 1])
        block_f = sb("block_f", [P, NODE_COLS + 1])
        block_i = sb("block_i", [P, NODE_COLS + 1], i32)
        inside = sb("inside", [P, NODE_COLS + 1])
        first = sb("first", [P, NODE_COLS + 1])
        last = sb("last", [P, NODE_COLS])
        last_i = sb("last_i", [P, NODE_COLS], i32)
        has = sb("has", [P, NODE_COLS])
        no_edge = sb("no_edge", [P, NODE_COLS])
        place = sb("place", [P, NODE_COLS])
        past = sb("past", [P, NODE_COLS])
        place_i = sb("place_i", [P, NODE_COLS], i32)
        crosses = sb("crosses", [P, STREAMS, NODE_COLS])
        crosses2 = sb("crosses2", [P, STREAMS, NODE_COLS])
        no_cross = sb("no_cross", [P, STREAMS, NODE_COLS])
        border = sb("border", [P, STREAMS, F])
        heads4 = sb("heads4", [STREAMS, 1], i32)
        rows4 = sb("rows4", [STREAMS, F])
        node_a = sb("node_a", [P, CHUNK, F])
        node_b = sb("node_b", [P, CHUNK, F])
        node_c = sb("node_c", [P, CHUNK, F])
        stat_a = sb("stat_a", [P, CHUNK])
        stat_b = sb("stat_b", [P, CHUNK])
        stat_c = sb("stat_c", [P, CHUNK])
        last_rows = sb("last_rows", [P, 2, CHUNK, 2 * F])

        src_idx = sb("src_idx", [P, PRE, SLOTS], i32)
        xg = sb("xg", [P, 2, SLOTS, 4 * F])
        xg0 = xg[:, :, :, :].rearrange("p a k (b f) -> p (a k b f)", f=F).rearrange(
            "p (u k f) -> p u k f", u=PRE, f=F)
        ea = sb("ea", [P, 2, LEN])
        sp_in = sb("sp_in", [P, 2, SLOTS, F])
        keep = sb("keep", [P, 4, LEN], bf16)
        fresh = sb("fresh", [P, 2, LEN], bf16)
        xt = sb("xt", [P, 2, LEN])
        dt_ = sb("dt_", [P, 2, LEN])
        hid = sb("hid", [P, 2, 2, LEN])
        scan = sb("scan", [P, 2, LEN])
        out0 = sb("out0", [P, 2, SLOTS, F])
        late = sb("late", [P, 15 * 1024])
        at = [0]

        def part(n):
            at[0] += n
            return late[:, at[0] - n:at[0]]
        x4 = part(2 * STREAMS * LEN).rearrange("p (u g n) -> p u g n", u=2, g=STREAMS)
        prod = part(G_BUFS * LEN).rearrange("p (b n) -> p b n", b=G_BUFS)
        types = part(STREAMS * LEN).bitcast(bf16).rearrange("p (u g n) -> p u g n", u=2, g=STREAMS)
        onehot = part(STREAMS * LEN).bitcast(bf16).rearrange("p (u g n) -> p u g n", u=2, g=STREAMS)
        out1 = part(2 * SLOTS * 2 * F).rearrange("p (u k f) -> p u k f", u=2, k=SLOTS)
        rows = late[:, 0:2 * SEARCH * BLOCK].rearrange("p (u t n) -> p u t n", u=2, t=SEARCH)
        ZERO = 4096
        zero = late[:, 15 * 1024 - ZERO:15 * 1024]
        comp = sb("comp", [P, 2, 2, LEN], bf16)
        query, score, wmsg = (hid[:, k // 2, k % 2, :] for k in range(3))
        weight = xt
        node_t = hid[:, 1, 1, :]

        bank = [ctx.enter_context(nc.psum_tensor(f"bank{i}", [P, 512], fp32)) for i in range(8)]

        loaded = sem("loaded")
        edges_in = sem("edges_in")
        filled = sem("filled")
        zeroed = sem("zeroed")
        parted = sem("parted")
        prepared = sem("prepared")
        prep_out = sem("prep_out")
        heads_ready = sem("heads_ready")
        sides = sem("sides")
        block_found = sem("block_found")
        rows_in = [sem(f"rows_in{u}") for u in range(2)]
        rows_used = sem("rows_used")
        placed = sem("placed")
        x_spread = sem("x_spread")
        ends_in = sem("ends_in")
        ends_out = sem("ends_out")
        dve_done = sem("dve_done")
        act_done = sem("act_done")
        rows_got = [[sem(f"rows_got{n}_{c}") for c in range(CHUNKS)] for n in range(2)]
        border_in = [sem(f"border_in{n}") for n in range(2)]
        centred = sem("centred")
        squared = sem("squared")
        var_ready = sem("var_ready")
        dev_ready = sem("dev_ready")
        node_ready = sem("node_ready")
        turned = sem("turned")
        turned_sb = sem("turned_sb")
        mapped = sem("mapped")
        y_ready = sem("y_ready")
        picked = sem("picked")
        added = sem("added")
        h_out = sem("h_out")
        y_out = sem("y_out")
        y_spread = sem("y_spread")
        result_out = sem("result_out")

        idx_in = [[sem(f"idx_in{n}_{u}") for u in range((PRE, 2)[n])] for n in range(2)]
        ea_in = [sem(f"ea_in{u}") for u in range(2)]
        types_in = [sem(f"types_in{u}") for u in range(2)]
        spread_in = [[sem(f"spread_in{n}_{u}") for u in range(2)] for n in range(2)]
        keep_in = [[sem(f"keep_in{n}_{u}") for u in range(4)] for n in range(2)]
        gathered = [[sem(f"gathered{n}_{u}") for u in range((PRE, 2)[n])] for n in range(2)]
        stored = [[sem(f"stored{n}_{u}") for u in range(2)] for n in range(2)]
        x_turned = [sem(f"x_turned{n}") for n in range(2)]
        x_ready = [sem(f"x_ready{n}") for n in range(2)]
        s_turned = [sem(f"s_turned{n}") for n in range(2)]
        d_ready = [sem(f"d_ready{n}") for n in range(2)]
        scanned = [sem(f"scanned{n}") for n in range(2)]
        o_turned = [sem(f"o_turned{n}") for n in range(2)]
        o_ready = [sem(f"o_ready{n}") for n in range(2)]
        fresh_ready = sem("fresh_ready")
        hid_done = sem("hid_done")
        relu_done = sem("relu_done")
        v_done = sem("v_done")
        onehot_ready = sem("onehot_ready")
        comp_done = sem("comp_done")
        comp_ready = sem("comp_ready")
        rel_done = sem("rel_done")
        key_done = sem("key_done")
        query_ready = sem("query_ready")
        score_ready = sem("score_ready")
        sum_done = sem("sum_done")
        weight_ready = sem("weight_ready")
        coef_done = sem("coef_done")
        prod_ready = sem("prod_ready")
        msg_done = sem("msg_done")
        wmsg_ready = sem("wmsg_ready")
        src_copied = sem("src_copied")

        waits_passed = {nc.sync: sem("sp_passed"), nc.gpsimd: sem("pool_passed")}
        N_CONST = 17
        block = ctx.enter_context(nc.Block())

        def wait_count(eng, s, semaphore, count):
            if s.known and count <= 0:
                return
            eng.wait_ge(semaphore, count)
            if not s.known and eng in waits_passed:
                eng.sem_inc(waits_passed[eng], 1)

        def wait_in(eng, s, semaphores, each=16):
            wait_count(eng, s, semaphores[s.slot(len(semaphores))], (s.earlier(len(semaphores)) + 1) * each)

        def wait_out(eng, s, semaphores, each=16):
            wait_count(eng, s, semaphores[s.slot(len(semaphores))], s.earlier(len(semaphores)) * each)

        def wait_step(eng, s, semaphore, each=1, lag=0, more=0):
            wait_count(eng, s, semaphore, (s.at - lag + 1) * each + more)

        spread_v = spread[0:EDGES, :].rearrange("(s p k) f -> s p k f", s=STEPS, p=P)
        spread_heads = spread[0:STREAMS, :]
        max_v = max_rows.rearrange("(s p k) f -> s p k f", s=STEPS, p=P)
        sum_v = sum_rows.rearrange("(s p k) f -> s p k f", s=STEPS, p=P)
        keep_v = keep_dram.rearrange("(g s n) -> s g n", g=STREAMS, s=STEPS)
        type_v = type_dram.rearrange("(g s n) -> s g n", g=STREAMS, s=STEPS)
        ea_v = t["edge_t"].rearrange("p (s n) -> s p n", s=STEPS)
        idx_v = t["src_t"]
        h_nodes = h_dram.rearrange("(p t) (c f) -> p t c f", p=P, f=F)
        y_nodes = y_dram.rearrange("(p t) f -> p t f", p=P)
        full = N_NODES // NODE_COLS
        tail = N_NODES - full * NODE_COLS
        out_full = t["out"][0:full * NODE_COLS, :].rearrange("(p t) f -> p t f", p=full)
        out_tail = t["out"][full * NODE_COLS:, :].rearrange("(p t) f -> p t f", p=1)

        def border_rows(eng, table, n):
            ends = table[EDGES - STREAMS:EDGES, 0:F]
            eng.dma_start(border[:, :, :], ends.partition_broadcast(P)).then_inc(border_in[n], 16)

        @block.sync
        def _(sp):
            def index_load0(s):
                wait_out(sp, s, gathered[0], 16 * SLOTS)
                sp.dma_start(src_idx[:, s.slot(PRE), :], idx_v[s.at]).then_inc(idx_in[0][s.slot(PRE)], 16)

            sp.dma_start(heads_i[:, :], t["heads"].partition_broadcast(P)).then_inc(edges_in, 16)
            sp.dma_start(dst_i, t["dst_rows"]).then_inc(edges_in, 16)
            sp.dma_start(prev_i, t["prev_rows"]).then_inc(edges_in, 16)
            sp.dma_start(type_i, t["type_rows"]).then_inc(edges_in, 16)
            sp.dma_start(heads4[:, :], t["heads4"]).then_inc(edges_in, 16)
            sp.dma_start(node_id[:, :], t["node_id"]).then_inc(edges_in, 16)
            sp.dma_start(node_half[:, :], t["node_half"]).then_inc(edges_in, 16)
            for off in range(PRE):
                index_load0(Step(PRE, 0, off))
            for tile, name in ((spare_id, "spare_id"), (row_id, "row_id"),
                               (ident, "ident"), (w1, "w1"), (w2, "w2"), (b1, "b1"), (a1w, "a1w"),
                               (a1b, "a1b"), (a2w, "a2w"), (self_w, "self_w"), (basis, "basis"),
                               (ones_blk, "ones_blk"), (sel_f, "sel"), (x, "x_nodes")):
                every = tuple(slice(None) for _ in tile.shape)
                sp.dma_start(tile[every], t[name]).then_inc(loaded, 16)
            sp.dma_start(b2[:, :], t["b2"].partition_broadcast(P)).then_inc(loaded, 16)
            sp.dma_start(a2b[:, :], t["a2b"].partition_broadcast(P)).then_inc(loaded, 16)
            sp.dma_start(rel[:, :], t["rel"]).then_inc(loaded, 16)
            sp.wait_ge(prepared, 3)
            sp.dma_start(dst_blocks.rearrange("a b -> (a b)").rearrange("(p n) -> p n", p=P),
                         dst_f).then_inc(prep_out, 16)
            sp.dma_start(keep_dram.rearrange("(p n) -> p n", p=P), keep_b).then_inc(prep_out, 16)
            sp.dma_start(type_dram.rearrange("(p n) -> p n", p=P), type_b).then_inc(prep_out, 16)
            sp.wait_ge(prep_out, 48)
            sp.wait_ge(ends_in, 16)
            sp.wait_ge(x_spread, 16 * NODE_COLS)
            sp.dma_start(spread_heads, rows4[:, :]).then_inc(ends_out, 16)
            sp.wait_ge(ends_out, 16)

            def keep_load(n, s):
                wait_step(sp, s, scanned[n], lag=4)
                for g in range(STREAMS):
                    sp.dma_start(keep[F * g:F * g + F, s.slot(4), :],
                                 keep_v[s.at][g].partition_broadcast(F)).then_inc(keep_in[n][s.slot(4)], 16)

            def loads0(s):
                index = s.plus(PRE - 2)
                if index.exists() and (not s.known or index.at >= PRE):
                    index_load0(index)
                wait_step(sp, s, s_turned[0], lag=2)
                sp.dma_start(sp_in[:, s.slot(2)], spread_v[s.at]).then_inc(spread_in[0][s.slot(2)], 16)
                wait_step(sp, s, hid_done, each=2, lag=2)
                sp.dma_start(ea[:, s.slot(2), :], ea_v[s.at]).then_inc(ea_in[s.slot(2)], 16)
                keep_load(0, s)

            run_steps(sp, loads0, PRE)

            for u in range(2):
                sp.wait_ge(stored[0][u], 16 * (STEPS // 2))
            border_rows(sp, max_rows, 0)
            for c in range(CHUNKS):
                cols = slice(c * CHUNK, (c + 1) * CHUNK)
                sp.wait_ge(node_ready, c + 1)
                for k in range(4):
                    sp.dma_start(h_nodes[:, cols, k, :], h[:, cols, :]).then_inc(h_out, 16)
                sp.wait_ge(y_ready, c + 1)
                sp.dma_start(y_nodes[:, cols, :], y[:, cols, :]).then_inc(y_out, 16)
            sp.wait_ge(ends_in, 32)
            sp.wait_ge(y_spread, 16 * NODE_COLS)
            sp.dma_start(spread_heads, rows4[:, :]).then_inc(ends_out, 16)
            sp.wait_ge(ends_out, 32)

            def loads1(s):
                wait_out(sp, s, gathered[1], 16 * SLOTS)
                sp.dma_start(src_idx[:, s.slot(2), :], idx_v[s.at]).then_inc(idx_in[1][s.slot(2)], 16)
                wait_step(sp, s, onehot_ready, lag=2)
                sp.dma_start(types[:, s.slot(2)], type_v[s.at].partition_broadcast(P)
                             ).then_inc(types_in[s.slot(2)], 16)
                wait_step(sp, s, s_turned[1], lag=2)
                sp.dma_start(sp_in[:, s.slot(2)], spread_v[s.at]).then_inc(spread_in[1][s.slot(2)], 16)
                keep_load(1, s)

            run_steps(sp, loads1, 4)

            for u in range(2):
                sp.wait_ge(stored[1][u], 16 * (STEPS // 2))
            border_rows(sp, sum_rows, 1)
            for c in range(CHUNKS):
                cols = slice(c * CHUNK, (c + 1) * CHUNK)
                sp.wait_ge(node_ready, CHUNKS + c + 1)
                sp.dma_start(out_full[:, cols, :], agg[0:full, cols, :]).then_inc(result_out, 16)
                got = min((c + 1) * CHUNK, tail) - c * CHUNK
                if got > 0:
                    cols = slice(c * CHUNK, c * CHUNK + got)
                    sp.dma_start(out_tail[:, cols, :], agg[full:full + 1, cols, :]).then_inc(result_out, 16)
            sp.wait_ge(result_out, 16 * (CHUNKS + -(-tail // CHUNK)))

        @block.gpsimd
        def _(pool):
            def gather(out, table, index, done):
                pool.indirect_dma_start(out=out, out_offset=None, in_=table,
                                        in_offset=bass.IndirectOffsetOnAxis(ap=index, axis=0)).then_inc(done, 16)

            def scatter(table, index, rows_, done):
                pool.indirect_dma_start(out=table, out_offset=bass.IndirectOffsetOnAxis(ap=index, axis=0),
                                        in_=rows_, in_offset=None).then_inc(done, 16)

            def gathers0(s):
                wait_in(pool, s, idx_in[0])
                wait_step(pool, s, x_turned[0], lag=PRE)
                for k in range(SLOTS):
                    gather(xg0[:, s.slot(PRE), k, :], t["x_dram"], src_idx[:, s.slot(PRE), k:k + 1],
                           gathered[0][s.slot(PRE)])

            pool.wait_ge(edges_in, 112)
            gather(rows4[:, :], t["x_dram"], heads4[:, :], ends_in)
            for off in range(PRE - SEARCHES // 2):
                gathers0(Step(PRE, 0, off))
            pool.wait_ge(prep_out, 48)
            for c in range(SEARCHES):
                pool.wait_ge(block_found, c + 1)
                if c >= 2:
                    pool.wait_ge(rows_used, c - 1)
                for k in range(c * SEARCH, min((c + 1) * SEARCH, NODE_COLS + 1)):
                    gather(rows[:, c % 2, k - c * SEARCH, :], dst_blocks, block_i[:, k:k + 1], rows_in[c % 2])
                if c % 2:
                    gathers0(Step(PRE, 0, PRE - SEARCHES // 2 + c // 2))
            pool.wait_ge(placed, 1)
            pool.wait_ge(loaded, 16 * N_CONST)
            pool.wait_ge(zeroed, 16 * N_ZERO)
            for k in range(NODE_COLS):
                scatter(spread, place_i[:, k:k + 1], x[:, k, :], x_spread)

            with pool.Fori(1, STEPS // PRE) as i:
                for off in range(PRE):
                    gathers0(Step(PRE, i, off))

            for u in range(2):
                pool.wait_ge(stored[0][u], 16 * (STEPS // 2))
            for c in range(CHUNKS):
                for k in range(c * CHUNK, (c + 1) * CHUNK):
                    gather(agg[:, k, :], max_rows, last_i[:, k:k + 1], rows_got[0][c])
            pool.wait_ge(ends_out, 16)
            for c in range(CHUNKS):
                pool.wait_ge(y_ready, c + 1)
                for k in range(c * CHUNK, (c + 1) * CHUNK):
                    scatter(spread, place_i[:, k:k + 1], y[:, k, :], y_spread)
            pool.wait_ge(y_out, 16 * CHUNKS)
            gather(rows4[:, :], y_dram, heads4[:, :], ends_in)
            pool.wait_ge(h_out, 4 * 16 * CHUNKS)

            def gathers1(s):
                wait_in(pool, s, idx_in[1])
                wait_step(pool, s, x_turned[1], each=STREAMS, lag=2)
                wait_step(pool, s, src_copied, lag=2)
                for k in range(SLOTS):
                    gather(xg[:, s.slot(2), k, :], h_dram, src_idx[:, s.slot(2), k:k + 1],
                           gathered[1][s.slot(2)])

            run_steps(pool, gathers1, 4)

            for u in range(2):
                pool.wait_ge(stored[1][u], 16 * (STEPS // 2))
            for c in range(CHUNKS):
                if c >= 2:
                    pool.wait_ge(added, c - 1)
                    pool.wait_ge(picked, c - 1)
                for k in range(CHUNK):
                    col = c * CHUNK + k
                    gather(last_rows[:, c % 2, k, :], sum_rows, last_i[:, col:col + 1], rows_got[1][c])

        @block.scalar
        def _(act):
            act.wait_ge(heads_ready, 1)
            for c in range(SEARCHES):
                for k in range(c * SEARCH, min((c + 1) * SEARCH, NODE_COLS + 1)):
                    if k >= 1:
                        act.wait_ge(sides, k)
                    act.activation(signs[:, 0:BLOCKS], heads[:, :], ACT.Sign, bias=node_half[:, k:k + 1],
                                   scale=-1.0, accum_out=side[:, k:k + 1]).then_inc(sides, 1)
                if c == 0:
                    act.wait_ge(filled, 3)
                    act.wait_ge(prep_out, 48)
                    flat = spread[0:EDGES, :].rearrange("e f -> (e f)")
                    for k in range(N_ZERO):
                        n = min(ZERO, EDGES * F // P - k * ZERO)
                        act.dma_start(flat[k * P * ZERO:k * P * ZERO + P * n].rearrange("(p n) -> p n", p=P),
                                      zero[:, 0:n]).then_inc(zeroed, 16)
            act.wait_ge(loaded, 16 * N_CONST)

            def store(n, s, tile, view):
                wait_step(act, s, o_ready[n])
                act.dma_start(view[s.at], tile).then_inc(stored[n][s.slot(2)], 16)

            def step0(s):
                u = s.slot(2)
                wait_step(act, s, x_turned[0])
                wait_step(act, s, hid_done, each=2, lag=2)
                act.copy(xt[:, u, :], bank[0][:, :]).then_inc(x_ready[0], 1)
                for q in range(2):
                    wait_step(act, s, hid_done, each=2, more=q - 1)
                    wait_step(act, s, v_done, lag=2)
                    act.activation(hid[:, u, q, :], bank[2 + q][:, :], ACT.Relu,
                                   bias=b1[:, 0:1]).then_inc(relu_done, 1)
                wait_step(act, s, o_turned[0])
                wait_out(act, s, stored[0])
                act.copy(out0[:, u].rearrange("p k f -> p (k f)"), bank[5][:, :]).then_inc(o_ready[0], 1)
                store(0, s, out0[:, u], max_v)

            run_steps(act, step0, PRE)

            def layer_norm(n):
                act.wait_ge(centred, n + 1)
                act.activation(node_c[:, :, :], node_b[:, :, :], ACT.Square).then_inc(squared, 1)
                act.wait_ge(var_ready, n + 1)
                act.activation(stat_b[:, :], stat_a[:, :], ACT.Sqrt, bias=eps[:, 0:1],
                               scale=1.0 / F).then_inc(dev_ready, 1)

            def turned_copy(n):
                act.wait_ge(turned, n + 1)
                if n > 0:
                    act.wait_ge(mapped, n)
                whole = P * sum(b - a == 4 for a, b in GROUPS)
                rest_rows = F * (CHUNK % 4)
                act.copy(node_t[:, 0:whole], bank[6][:, 0:whole])
                act.copy(node_t[0:rest_rows, whole:whole + P],
                         bank[6][0:rest_rows, whole:whole + P]).then_inc(turned_sb, 1)

            for c in range(CHUNKS):
                layer_norm(c)
                turned_copy(c)

            def comp_copies(s):
                for q in range(2):
                    wait_step(act, s, comp_done)
                    wait_step(act, s, coef_done, each=SLOTS, lag=2)
                    act.copy(comp[:, s.slot(2), q, :], bank[q][:, :]).then_inc(comp_ready, 1)

            def x4_copy(s, g):
                wait_step(act, s, x_turned[1], each=STREAMS, more=g - 3)
                wait_step(act, s, prod_ready, each=SLOTS, lag=2)
                wait_step(act, s, key_done, lag=2)
                act.copy(x4[:, s.slot(2), g, :], bank[g % 2][:, :]).then_inc(x_ready[1], 1)

            def attend(s):
                wait_step(act, s, sum_done)
                wait_step(act, s, wmsg_ready, lag=2)
                act.activation(weight[:, s.slot(2), :], bank[1][:, :], ACT.Tanh, scale=float(F) ** -0.5
                               ).then_inc(weight_ready, 1)

            def src_copy(s):
                wait_in(act, s, gathered[1], 16 * SLOTS)
                wait_out(act, s, stored[1])
                act.copy(out1[:, s.slot(2), :, F:2 * F], xg[:, s.slot(2), :, 0:F]).then_inc(src_copied, 1)

            def finish(s):
                wait_step(act, s, o_turned[1])
                act.copy(out1[:, s.slot(2), :, 0:F], bank[4][:, :].rearrange("p (k f) -> p k f", f=F)
                         ).then_inc(o_ready[1], 1)
                wait_step(act, s, src_copied)
                store(1, s, out1[:, s.slot(2)], sum_v)

            def step1(s):
                ahead, behind = s.plus(1), s.plus(-1)
                attend(s)
                if ahead.exists():
                    comp_copies(ahead)
                src_copy(s)
                if ahead.exists():
                    for g in range(STREAMS):
                        x4_copy(ahead, g)
                if behind.exists():
                    finish(behind)

            comp_copies(Step(4, 0, 0))
            for g in range(STREAMS):
                x4_copy(Step(4, 0, 0), g)
            run_steps(act, step1, 4)
            finish(Step(4, 0, STEPS - 1))

            for c in range(CHUNKS):
                act.wait_ge(rows_got[1][c], 16 * CHUNK)
                if c > 0:
                    act.wait_ge(turned, CHUNKS + c)
                act.copy(y[:, 0:CHUNK, :], last_rows[:, c % 2, :, F:2 * F]).then_inc(picked, 1)
                turned_copy(CHUNKS + c)
                layer_norm(CHUNKS + c)

        @block.vector
        def _(dve):
            done = [0]

            def link(ins):
                done[0] += 1
                ins.then_inc(dve_done, 1)
                dve.wait_ge(dve_done, done[0])

            dve.memset(zero, 0.0).then_inc(filled, 1)
            dve.memset(eps[:, :], EPS).then_inc(filled, 1)
            dve.memset(rest[:, :], 0.0).then_inc(filled, 1)
            dve.memset(comp_lhs[:, :], 0.0).then_inc(filled, 1)
            dve.wait_ge(edges_in, 112)
            dve.tensor_copy(heads[:, :], heads_i[:, :]).then_inc(heads_ready, 1)
            dve.tensor_copy(dst_f, dst_i).then_inc(prepared, 1)
            dve.tensor_tensor(keep_b, dst_i, prev_i, ALU.is_equal).then_inc(prepared, 1)
            dve.tensor_copy(type_b, type_i).then_inc(prepared, 1)

            def find_blocks(c):
                cols = slice(c * SEARCH, min((c + 1) * SEARCH, NODE_COLS + 1))
                dve.wait_ge(sides, cols.stop)
                link(dve.tensor_scalar(block_f[:, cols], side[:, cols], 0.5, 0.5 * BLOCKS - 1.0, ALU.mult,
                                       ALU.add))
                link(dve.tensor_scalar(block_f[:, cols], block_f[:, cols], 0.0, None, ALU.max))
                dve.tensor_copy(block_i[:, cols], block_f[:, cols]).then_inc(block_found, 1)

            def find_edges(c):
                cols = slice(c * SEARCH, min((c + 1) * SEARCH, NODE_COLS + 1))
                got = sum(len(range(d * SEARCH, min((d + 1) * SEARCH, NODE_COLS + 1)))
                          for d in range(c % 2, c + 1, 2))
                dve.wait_ge(rows_in[c % 2], 16 * got)
                for k in range(cols.start, cols.stop):
                    link(dve.tensor_scalar(below[:, :], rows[:, c % 2, k - cols.start, :], node_id[:, k:k + 1],
                                           None, ALU.is_lt, ALU.add, accum_out=inside[:, k:k + 1]))
                dve.scalar_tensor_tensor(first[:, cols], block_f[:, cols], float(BLOCK), inside[:, cols],
                                         ALU.mult, ALU.add).then_inc(rows_used, 1)

            find_blocks(0)
            for c in range(SEARCHES):
                if c + 1 < SEARCHES:
                    find_blocks(c + 1)
                find_edges(c)
            dve.wait_ge(rows_used, SEARCHES)
            dve.wait_ge(loaded, 16 * N_CONST)
            begin, end = first[:, 0:NODE_COLS], first[:, 1:NODE_COLS + 1]
            link(dve.tensor_tensor(has[:, :], end, begin, ALU.is_gt))
            link(dve.tensor_scalar(last[:, :], end, -1.0, 0.0, ALU.add, ALU.max))

            def table_row(edge, out):
                link(dve.tensor_scalar(out, edge, float(STREAMS), None, ALU.mult))
                for g in range(1, STREAMS):
                    link(dve.tensor_scalar(past[:, :], edge, float(g * STREAM), float(1 - EDGES), ALU.is_ge,
                                           ALU.mult))
                    link(dve.tensor_tensor(out, out, past[:, :], ALU.add))

            table_row(last[:, :], place[:, :])
            link(dve.tensor_copy(last_i[:, :], place[:, :]))
            table_row(begin, place[:, :])
            link(dve.tensor_tensor(place[:, :], place[:, :], spare_id[:, :], ALU.subtract))
            link(dve.tensor_tensor(place[:, :], place[:, :], has[:, :], ALU.mult))
            link(dve.tensor_tensor(place[:, :], place[:, :], spare_id[:, :], ALU.add))
            dve.tensor_copy(place_i[:, :], place[:, :]).then_inc(placed, 1)
            link(dve.tensor_scalar(no_edge[:, :], has[:, :], -1.0, BIG, ALU.add, ALU.mult))
            for g in range(1, STREAMS):
                link(dve.tensor_scalar(crosses2[:, g, :], begin, float(g * STREAM), None, ALU.is_lt))
                link(dve.tensor_scalar(crosses[:, g, :], last[:, :], float(g * STREAM), None, ALU.is_ge))
                link(dve.tensor_tensor(crosses[:, g, :], crosses[:, g, :], crosses2[:, g, :], ALU.mult))
                link(dve.tensor_scalar(no_cross[:, g, :], crosses[:, g, :], -1.0, BIG, ALU.add, ALU.mult))

            dve.wait_ge(loaded, 16 * N_CONST)
            link(dve.tensor_copy(rel_parts[:, 0, :], rel[:, :]))
            link(dve.tensor_tensor(rest[:, :], rel[:, :], rel_parts[:, 0, :], ALU.subtract))
            link(dve.tensor_copy(rel_parts[:, 1, :], rest[:, :]))
            link(dve.tensor_tensor(rest2[:, :], rest[:, :], rel_parts[:, 1, :], ALU.subtract))
            link(dve.tensor_copy(rel_parts[:, 2, :], rest2[:, :]))
            for q in range(PARTS):
                link(dve.tensor_copy(comp_lhs[:, q * BASES:(q + 1) * BASES], rel_parts[:, q, F:F + BASES]))
            dve.tensor_copy(sel[:, :, :], sel_f[:, :, :]).then_inc(parted, 1)

            def before(s, tile, start=0.0):
                u = s.slot(2)
                return start if s.known and s.at == 0 else tile[:, 1 - u, LEN - 1:LEN]

            def spread_scan(n, s, b):
                wait_in(dve, s, keep_in[n], 16 * STREAMS)
                wait_step(dve, s, s_turned[n])
                wait_step(dve, s, d_ready[n], lag=1)
                dve.tensor_tensor_scan(dt_[:, s.slot(2), :], keep[:, s.slot(4), :], bank[b][:, :],
                                       before(s, dt_), ALU.mult, ALU.add).then_inc(d_ready[n], 1)

            def step0(s):
                u = s.slot(2)
                wait_step(dve, s, hid_done, each=2, lag=2)
                spread_scan(0, s, 1)
                wait_step(dve, s, scanned[0], lag=2)
                dve.tensor_scalar(fresh[:, u, :], keep[:, s.slot(4), :], -1.0, BIG, ALU.add, ALU.mult
                                  ).then_inc(fresh_ready, 1)
                wait_step(dve, s, v_done)
                wait_step(dve, s, fresh_ready)
                wait_step(dve, s, o_turned[0], lag=2)
                wait_step(dve, s, scanned[0], lag=1)
                dve.tensor_tensor_scan(scan[:, u, :], fresh[:, u, :], bank[4][:, :], before(s, scan, -BIG),
                                       ALU.add, ALU.max).then_inc(scanned[0], 1)

            run_steps(dve, step0, PRE)

            shape = [P, CHUNK, F]

            def layer_norm(n, out):
                link(dve.tensor_reduce(stat_a[:, :], node_a[:, :, :], AX.X, ALU.add))
                link(dve.tensor_scalar(stat_c[:, :], stat_a[:, :], 1.0 / F, None, ALU.mult))
                dve.tensor_tensor(node_b[:, :, :], node_a[:, :, :], bc(stat_c[:, :], shape, 2), ALU.subtract
                                  ).then_inc(centred, 1)
                dve.wait_ge(centred, n + 1)
                dve.wait_ge(squared, n + 1)
                dve.tensor_reduce(stat_a[:, :], node_c[:, :, :], AX.X, ALU.add).then_inc(var_ready, 1)
                dve.wait_ge(dev_ready, n + 1)
                link(dve.reciprocal(stat_c[:, :], stat_b[:, :]))
                dve.tensor_tensor(out, node_b[:, :, :], bc(stat_c[:, :], shape, 2), ALU.mult
                                  ).then_inc(node_ready, 1)
                dve.wait_ge(node_ready, n + 1)

            dve.wait_ge(border_in[0], 16)
            for c in range(CHUNKS):
                cols = slice(c * CHUNK, (c + 1) * CHUNK)
                dve.wait_ge(rows_got[0][c], 16 * CHUNK)
                v = agg[:, cols, :]
                for g in range(1, STREAMS):
                    link(dve.tensor_tensor(node_b[:, :, :], bc(border[:, g - 1, :], shape, 1),
                                           bc(no_cross[:, g, cols], shape, 2), ALU.add))
                    link(dve.tensor_tensor(v, v, node_b[:, :, :], ALU.max))
                link(dve.tensor_tensor(v, v, bc(b2[:, :], shape, 1), ALU.add))
                link(dve.tensor_tensor(v, v, bc(no_edge[:, cols], shape, 2), ALU.add))
                link(dve.tensor_tensor(v, v, x[:, cols, :], ALU.max))
                link(dve.tensor_tensor(node_a[:, :, :], v, x[:, cols, :], ALU.add))
                layer_norm(c, h[:, cols, :])
                dve.wait_ge(mapped, c + 1)
                dve.tensor_tensor(y[:, cols, :], bank[7][:, 0:CHUNK * F].rearrange("p (t f) -> p t f", f=F),
                                  bc(a2b[:, :], shape, 1), ALU.add).then_inc(y_ready, 1)

            def one_hot(s):
                wait_in(dve, s, types_in)
                wait_step(dve, s, rel_done, lag=2)
                dve.tensor_scalar(onehot[:, s.slot(2), :, :], types[:, s.slot(2), :, :], row_id[:, 0:1], None,
                                  ALU.is_equal).then_inc(onehot_ready, 1)

            def find_query(s):
                wait_step(dve, s, d_ready[1])
                wait_step(dve, s, rel_done)
                wait_step(dve, s, score_ready, lag=1)
                dve.tensor_tensor(query, dt_[:, s.slot(2), :], bank[5][:, :], ALU.add).then_inc(query_ready, 1)

            def find_score(s):
                wait_step(dve, s, query_ready)
                wait_step(dve, s, key_done)
                wait_step(dve, s, sum_done, lag=1)
                dve.scalar_tensor_tensor(score, bank[0][:, :], a1b[:, 0:1], query, ALU.add, ALU.mult
                                         ).then_inc(score_ready, 1)

            def product(s, n):
                k, g = divmod(n, STREAMS)
                wait_step(dve, s, coef_done, each=SLOTS, more=n - SLOTS + 1)
                wait_step(dve, s, x_ready[1], each=STREAMS, more=g - 3)
                wait_step(dve, s, msg_done, each=KCH, more=k - 3 - G_BUFS // STREAMS)
                dve.tensor_tensor(prod[:, n % G_BUFS, :], x4[:, s.slot(2), g, :],
                                  bank[C_BANK[n]][:, :], ALU.mult).then_inc(prod_ready, 1)

            def weigh(s):
                wait_step(dve, s, msg_done, each=KCH)
                wait_step(dve, s, weight_ready)
                wait_step(dve, s, scanned[1], lag=1)
                dve.scalar_tensor_tensor(wmsg, weight[:, s.slot(2), :], 0.0, bank[7][:, :], ALU.max, ALU.mult
                                         ).then_inc(wmsg_ready, 1)

            def sum_scan(s):
                wait_step(dve, s, wmsg_ready)
                wait_step(dve, s, o_turned[1], lag=2)
                dve.tensor_tensor_scan(scan[:, s.slot(2), :], keep[:, s.slot(4), :], wmsg, before(s, scan),
                                       ALU.mult, ALU.add).then_inc(scanned[1], 1)

            def step1(s):
                for n in range(SLOTS):
                    product(s, n)
                    if n == 3 and s.plus(-1).exists():
                        weigh(s.plus(-1))
                    if n == 4 and s.plus(-1).exists():
                        sum_scan(s.plus(-1))
                    if n == 5 and s.plus(2).exists():
                        one_hot(s.plus(2))
                    if n == 7 and s.plus(1).exists():
                        spread_scan(1, s.plus(1), 4)
                    if n == 8 and s.plus(1).exists():
                        find_query(s.plus(1))
                    if n == 13 and s.plus(1).exists():
                        find_score(s.plus(1))

            first_step = Step(4, 0, 0)
            one_hot(first_step)
            one_hot(first_step.plus(1))
            spread_scan(1, first_step, 4)
            find_query(first_step)
            find_score(first_step)
            run_steps(dve, step1, 4)
            weigh(Step(4, 0, STEPS - 1))
            sum_scan(Step(4, 0, STEPS - 1))

            dve.wait_ge(border_in[1], 16)
            for c in range(CHUNKS):
                cols = slice(c * CHUNK, (c + 1) * CHUNK)
                dve.wait_ge(rows_got[1][c], 16 * CHUNK)
                v = agg[:, cols, :]
                nei = last_rows[:, c % 2, :, 0:F]
                for g in range(1, STREAMS):
                    link(dve.tensor_tensor(node_b[:, :, :], bc(border[:, g - 1, :], shape, 1),
                                           bc(crosses[:, g, cols], shape, 2), ALU.mult))
                    link(dve.tensor_tensor(v, nei if g == 1 else v, node_b[:, :, :], ALU.add))
                dve.wait_ge(mapped, CHUNKS + c + 1)
                dve.tensor_tensor(node_a[:, :, :], v, bank[7][:, 0:CHUNK * F].rearrange("p (t f) -> p t f", f=F),
                                  ALU.add).then_inc(added, 1)
                dve.wait_ge(added, c + 1)
                link(dve.tensor_tensor(node_b[:, :, :], node_a[:, :, :], bc(has[:, cols], shape, 2), ALU.mult))
                link(dve.scalar_tensor_tensor(node_a[:, :, :], node_b[:, :, :], 0.0, h[:, cols, :],
                                              ALU.max, ALU.add))
                layer_norm(CHUNKS + c, v)

        @block.tensor
        def _(pe):
            pe.wait_ge(loaded, 16 * N_CONST)
            pe.wait_ge(parted, 1)

            def spread_turn(n, s, b):
                wait_in(pe, s, spread_in[n])
                out = bank[b][:, :].rearrange("p (n j) -> p j n", j=TILES)
                for j in range(TILES):
                    last_ = pe.transpose(out[:, j, :], sp_in[:, s.slot(2), j * STREAMS:(j + 1) * STREAMS, :],
                                         ident[:, :])
                last_.then_inc(s_turned[n], 1)

            def scan_turn(n, s, b):
                wait_step(pe, s, scanned[n])
                wait_step(pe, s, o_ready[n], lag=1)
                src = scan[:, s.slot(2), :].rearrange("p (n j) -> p j n", j=TILES)
                for j in range(TILES):
                    last_ = pe.transpose(bank[b][:, P * j:P * j + P], src[:, j, :], ident[:, :])
                last_.then_inc(o_turned[n], 1)

            def step0(s):
                u = s.slot(2)
                wait_in(pe, s, gathered[0], 16 * SLOTS)
                wait_step(pe, s, x_ready[0], lag=1)
                out = bank[0][:, :].rearrange("p (n j) -> p j n", j=TILES)
                for j in range(TILES):
                    last_ = pe.transpose(out[:, j, :], xg0[:, s.slot(PRE), j * STREAMS:(j + 1) * STREAMS, :],
                                         ident[:, :])
                last_.then_inc(x_turned[0], 1)
                wait_step(pe, s, d_ready[0], lag=1)
                spread_turn(0, s, 1)
                wait_step(pe, s, x_ready[0])
                wait_in(pe, s, ea_in)
                for q in range(2):
                    wait_step(pe, s, relu_done, each=2, lag=1, more=q - 1)
                    for k, rhs in enumerate((xt, ea, dt_)):
                        if rhs is dt_:
                            wait_step(pe, s, d_ready[0])
                        last_ = pe.matmul(bank[2 + q][:, :], w1[:, (0, 2, 1)[k], q, :], rhs[:, u, :],
                                          start=k == 0, stop=k == 2)
                    last_.then_inc(hid_done, 1)
                wait_step(pe, s, scanned[0], lag=1)
                for q in range(2):
                    wait_step(pe, s, relu_done, each=2, more=q - 1)
                    last_ = pe.matmul(bank[4][:, :], w2[:, q, :], hid[:, u, q, :], start=q == 0, stop=q == 1)
                last_.then_inc(v_done, 1)
                scan_turn(0, s, 5)

            run_steps(pe, step0, PRE)

            def node_map(n, source, weights):
                if n > 0:
                    pe.wait_ge(turned_sb, n)
                for k, (a, b) in enumerate(GROUPS):
                    m = F * (b - a)
                    last_ = pe.transpose(bank[6][0:m, P * k:P * k + P], source[:, a:b, :], ident[:, :])
                last_.then_inc(turned, 1)
                pe.wait_ge(turned_sb, n + 1)
                for k, (a, b) in enumerate(GROUPS):
                    m = F * (b - a)
                    last_ = pe.matmul(bank[7][:, F * a:F * b], node_t[0:m, P * k:P * k + P],
                                      weights[0:m, 0:m], start=True, stop=True)
                last_.then_inc(mapped, 1)

            for c in range(CHUNKS):
                pe.wait_ge(node_ready, c + 1)
                if c > 0:
                    pe.wait_ge(y_ready, c)
                node_map(c, h[:, c * CHUNK:(c + 1) * CHUNK, :], a2w)

            def coef(s, n):
                k, g = divmod(n, STREAMS)
                wait_step(pe, s, prod_ready, each=SLOTS, lag=1, more=C_FREE[n])
                pe.matmul(bank[C_BANK[n]][:, :], sel[:, (g % 2) * KCH + k, :], comp[:, s.slot(2), g // 2, :],
                          start=True, stop=True).then_inc(coef_done, 1)

            def messages(s, k):
                wait_step(pe, s, prod_ready, each=SLOTS, more=(k + 1) * STREAMS - SLOTS)
                if k == 0:
                    wait_step(pe, s, wmsg_ready, lag=1)
                for g in range(STREAMS):
                    last_ = pe.matmul(bank[7][F * g:F * g + F, :], basis[:, k, :],
                                      prod[:, (k * STREAMS + g) % G_BUFS, :], start=k == 0, stop=k == KCH - 1,
                                      tile_position=(0, F * g))
                last_.then_inc(msg_done, 1)

            def score_sum(s):
                wait_step(pe, s, score_ready)
                pe.matmul(bank[1][:, :], ones_blk[:, :], score, start=True, stop=True).then_inc(sum_done, 1)

            def compose(s):
                wait_step(pe, s, onehot_ready)
                wait_step(pe, s, score_ready, lag=1)
                wait_step(pe, s, weight_ready, lag=1)
                for g in range(STREAMS):
                    o = 64 * (g % 2)
                    last_ = pe.matmul(bank[g // 2][o:o + 64, :], comp_lhs[:, :], onehot[:, s.slot(2), g, :],
                                      start=True, stop=True, tile_position=(0, o))
                last_.then_inc(comp_done, 1)

            def relate(s):
                wait_step(pe, s, onehot_ready)
                wait_step(pe, s, query_ready, lag=1)
                for q in range(PARTS):
                    for g in range(STREAMS):
                        last_ = pe.matmul(bank[5][F * g:F * g + F, :], rel_parts[:, q, 0:F],
                                          onehot[:, s.slot(2), g, :], start=q == 0, stop=q == PARTS - 1,
                                          tile_position=(0, F * g))
                last_.then_inc(rel_done, 1)

            def source_turn(s, g):
                if g == 0:
                    wait_in(pe, s, gathered[1], 16 * SLOTS)
                if g < 2:
                    wait_step(pe, s, comp_ready, each=2, more=g - 1)
                else:
                    wait_step(pe, s, x_ready[1], each=STREAMS, more=g - 2 - 3)
                out = bank[g % 2][:, :].rearrange("p (n j) -> p j n", j=TILES)
                for j in range(TILES):
                    last_ = pe.transpose(out[:, j, :], xg[:, s.slot(2), j * STREAMS + g, :], ident[:, :])
                last_.then_inc(x_turned[1], 1)

            def find_key(s):
                wait_step(pe, s, x_ready[1], each=STREAMS)
                for g in range(STREAMS):
                    last_ = pe.matmul(bank[0][F * g:F * g + F, :], a1w[:, :], x4[:, s.slot(2), g, :],
                                      start=True, stop=True, tile_position=(0, F * g))
                last_.then_inc(key_done, 1)

            def step1(s):
                ahead, behind = s.plus(1), s.plus(-1)
                for n in range(SLOTS):
                    coef(s, n)
                    if n == 0:
                        score_sum(s)
                    if n == 1 and behind.exists():
                        messages(behind, KCH - 1)
                    if n in (7, 10, 14):
                        messages(s, (n - 7 + 1) // 3)
                    if n == 12 and behind.exists():
                        scan_turn(1, behind, 4)
                    if ahead.exists():
                        if n == 2:
                            relate(ahead)
                        if n == 3:
                            compose(ahead)
                        if n == 4:
                            wait_step(pe, s, o_ready[1], lag=2)
                            spread_turn(1, ahead, 4)
                        if n in (5, 6, 8, 9):
                            source_turn(ahead, (5, 6, 8, 9).index(n))
                        if n == 11:
                            find_key(ahead)

            first_step = Step(4, 0, 0)
            relate(first_step)
            compose(first_step)
            spread_turn(1, first_step, 4)
            for g in range(STREAMS):
                source_turn(first_step, g)
            find_key(first_step)
            run_steps(pe, step1, 4)
            messages(Step(4, 0, STEPS - 1), KCH - 1)
            scan_turn(1, Step(4, 0, STEPS - 1), 4)

            for c in range(CHUNKS):
                pe.wait_ge(picked, c + 1)
                if c > 0:
                    pe.wait_ge(added, c)
                node_map(CHUNKS + c, y[:, 0:CHUNK, :], self_w)


N_ZERO = -(-(EDGES * F) // (P * 4096))


def _blocks(a, n):
    r, c = a.shape
    out = np.zeros((n * r, n * c), a.dtype)
    for i in range(n):
        out[i * r:(i + 1) * r, i * c:(i + 1) * c] = a
    return out


def kernel(x, src, dst, edge_attr_32, edge_type_86, L0_gnn_W1, L0_gnn_b1, L0_gnn_W2, L0_gnn_b2,
           L1_gnn_weight, L1_gnn_w_comp, L1_gnn_self_loop_weight, L1_gnn_A1_w, L1_gnn_A1_b,
           L1_gnn_A2_w, L1_gnn_A2_b, L1_gnn_rel_emb):
    from concourse import bacc
    from concourse.bass_utils import run_bass_kernel_spmd

    f32 = np.float32
    xs, src, dst, types, attr = (np.asarray(a) for a in (x, src, dst, edge_type_86, edge_attr_32))
    pad = EDGES - N_EDGES
    x_pad = np.concatenate([xs, np.zeros((NODES - N_NODES, F), f32)])
    src_pad = np.concatenate([src, np.zeros(pad, src.dtype)])
    dst_pad = np.concatenate([dst, np.full(pad, NODES, dst.dtype)])
    type_pad = np.concatenate([types, np.zeros(pad, types.dtype)])
    attr_pad = np.concatenate([attr, np.zeros((pad, F), f32)])
    prev = np.concatenate([np.full(1, -1, dst.dtype), dst_pad[:-1]])

    W1 = np.asarray(L0_gnn_W1).reshape(3, F, HID)
    w1 = np.zeros((P, 3, 2, P), f32)
    w2 = np.zeros((P, 2, P), f32)
    for g in range(STREAMS):
        q, o = g // 2, HID * (g % 2)
        w1[F * g:F * g + F, :, q, o:o + HID] = W1.transpose(1, 0, 2)
        w2[o:o + HID, q, F * g:F * g + F] = np.asarray(L0_gnn_W2)
    sel = np.zeros((2, 64, 2, KCH, 4, F), f32)
    for half in range(2):
        for q in range(PARTS):
            for k in range(KCH):
                for b in range(4):
                    sel[half, q * BASES + 4 * k + b, half, k, b, :] = 1.0
    rel = np.zeros((P, F + BASES), f32)
    n_types = np.asarray(L1_gnn_rel_emb).shape[0]
    rel[:n_types, :F] = np.asarray(L1_gnn_rel_emb)
    rel[:n_types, F:] = np.asarray(L1_gnn_w_comp)
    nodes = (np.arange(P)[:, None] * NODE_COLS + np.arange(NODE_COLS + 1)[None, :]).astype(f32)

    arrays = {
        "x_dram": x_pad,
        "x_nodes": x_pad.reshape(P, NODE_COLS, F),
        "src_t": src_pad.reshape(STREAMS, STEPS, P, TILES).transpose(1, 2, 3, 0).reshape(STEPS, P, SLOTS),
        "dst_rows": dst_pad.reshape(P, ROW),
        "prev_rows": prev.reshape(P, ROW),
        "type_rows": type_pad.reshape(P, ROW),
        "heads": dst_pad[::BLOCK],
        "heads4": dst_pad[::STREAM].reshape(STREAMS, 1),
        "edge_t": attr_pad.reshape(STREAMS, STREAM, F).transpose(0, 2, 1).reshape(P, STREAM),
        "w1": w1,
        "w2": w2,
        "b1": np.tile(np.asarray(L0_gnn_b1), 2).reshape(P, 1),
        "b2": np.asarray(L0_gnn_b2),
        "a1w": np.concatenate([np.asarray(L1_gnn_A1_w).T, np.zeros((P - F, F), f32)]),
        "a1b": np.tile(np.asarray(L1_gnn_A1_b), 4).reshape(P, 1),
        "a2w": _blocks(np.asarray(L1_gnn_A2_w).T, 4),
        "a2b": np.asarray(L1_gnn_A2_b),
        "self_w": _blocks(np.asarray(L1_gnn_self_loop_weight), 4),
        "basis": np.asarray(L1_gnn_weight).reshape(KCH, P, F).transpose(1, 0, 2),
        "rel": rel,
        "ident": np.eye(P, dtype=f32),
        "ones_blk": _blocks(np.ones((F, F), f32), 4),
        "sel": sel.reshape(P, 2 * KCH, P),
        "row_id": np.arange(P, dtype=f32).reshape(P, 1),
        "node_id": nodes,
        "node_half": nodes - 0.5,
        "spare_id": nodes[:, :NODE_COLS] + EDGES,
    }
    arrays = {k: np.ascontiguousarray(a) for k, a in arrays.items()}

    nc = bacc.Bacc("TRN2", target_bir_lowering=False, num_devices=1)
    t = {k: nc.dram_tensor("in_" + k, a.shape, mybir.dt.from_np(a.dtype), kind="ExternalInput").ap()
         for k, a in arrays.items()}
    t["out"] = nc.dram_tensor("out", (N_NODES, F), fp32, kind="ExternalOutput").ap()
    build(nc, t)
    r = run_bass_kernel_spmd(nc, [{"in_" + k: a for k, a in arrays.items()}], core_ids=[0])
    return r.results[0]["out"]
```

```python
from contextlib import ExitStack

import numpy as np

import concourse.bass as bass
from concourse import mybir

P = 128
N_NODES, N_EDGES = 12500, 212500
F = 32
HID = 64
BASES = 16
STREAMS = 4
LEN = 512
TILES = LEN // P
SLOTS = STREAMS * TILES
STEPS = -(-N_EDGES // (STREAMS * LEN))
STEPS += -STEPS % 8
STREAM = STEPS * LEN
EDGES = STREAMS * STREAM
ROW = EDGES // P
NODE_COLS = -(-N_NODES // P)
NODES = P * NODE_COLS
CHUNK = 14
CHUNKS = NODE_COLS // CHUNK
GROUPS = [(a, min(a + 4, CHUNK)) for a in range(0, CHUNK, 4)]
SHIFT = 16384
SEARCH = 11
SEARCHES = (NODE_COLS + 1) // SEARCH
EARLY_COLS = 5 * SEARCH - 1
HALVES = [(0, 1024), (1024, ROW)]
PARTS = 3
KCH = BASES // 4
BIG = 3.0e38
EPS = 1e-5
PRE = 8
C_BANK = [(2, 3, 6)[n % 3] for n in range(SLOTS - 1)] + [3]
C_FREE = [max(m for m in range(-SLOTS, n) if C_BANK[m % SLOTS] == C_BANK[n]) + 1 for n in range(SLOTS)]
G_BUFS = 8
TURNS = ((5, 6, 8, 9), 11, 0)
LATE_TURNS = ((9, 11, 13, 14), 15, 2)

ZERO = 2 * ROW
N_ZERO = EDGES * F // (P * ZERO)
LATE = 2 * STREAMS * LEN + G_BUFS * LEN + 2 * STREAMS * LEN
LATE = max(LATE, ZERO + 3 * ROW + ROW + 1 + (NODE_COLS + 1) * P // 2)

fp32, bf16, i32 = mybir.dt.float32, mybir.dt.bfloat16, mybir.dt.int32
ALU = mybir.AluOpType
ACT = mybir.ActivationFunctionType
AX = mybir.AxisListType


def bc(ap, shape, axis):
    return ap.unsqueeze(axis).broadcast_to(shape)


class Step:

    def __init__(self, unroll, i, off):
        self.unroll, self.i, self.off = unroll, i, off
        self.known = isinstance(i, int)
        self.at = i * unroll + off

    def plus(self, n):
        return Step(self.unroll, self.i, self.off + n)

    def slot(self, n):
        return self.off % n

    def earlier(self, n):
        return self.i * (self.unroll // n) + self.off // n

    def exists(self):
        return not self.known or 0 <= self.at < STEPS


def run_steps(eng, body, unroll):
    for off in range(unroll):
        body(Step(unroll, 0, off))
    with eng.Fori(1, STEPS // unroll - 1) as i:
        for off in range(unroll):
            body(Step(unroll, i, off))
    for off in range(unroll):
        body(Step(unroll, STEPS // unroll - 1, off))


def build(nc, t):
    ctx = ExitStack()
    with ctx:
        def sb(name, shape, dt=fp32):
            return ctx.enter_context(nc.sbuf_tensor(name, shape, dt))

        def dram(name, shape, dt=fp32):
            return nc.dram_tensor(name, shape, dt, kind="Internal").ap()

        def sem(name):
            return ctx.enter_context(nc.semaphore(name))

        keep_dram = dram("keep_dram", [EDGES], bf16)
        type_dram = dram("type_dram", [EDGES], bf16)
        spread = dram("spread", [EDGES + NODES, F])
        max_rows = dram("max_rows", [EDGES, F])
        sum_rows = dram("sum_rows", [EDGES, 2 * F])
        h_dram = dram("h_dram", [NODES, 4 * F])
        y_dram = dram("y_dram", [NODES, F])

        ident = sb("ident", [P, P])
        w1 = sb("w1", [P, 3, 2, P])
        w2 = sb("w2", [P, 2, P])
        b1 = sb("b1", [P, 1])
        b2 = sb("b2", [P, F])
        a1w = sb("a1w", [P, F])
        a1b = sb("a1b", [P, 1])
        a2w = sb("a2w", [P, P])
        a2b = sb("a2b", [P, F])
        self_w = sb("self_w", [P, P])
        basis = sb("basis", [P, KCH, F])
        ones_blk = sb("ones_blk", [P, P])
        sel = sb("sel", [P, 2 * KCH, P], bf16)
        rel = sb("rel", [P, F + BASES])
        rest = sb("rest", [P, F + BASES])
        rest2 = sb("rest2", [P, F + BASES])
        rel_parts = sb("rel_parts", [P, PARTS, F + BASES], bf16)
        comp_lhs = sb("comp_lhs", [P, 64], bf16)
        row_id = sb("row_id", [P, 1])
        node_half = sb("node_half", [P, NODE_COLS + 1])
        spare_id = sb("spare_id", [P, NODE_COLS])
        eps = sb("eps", [P, 1])

        x = sb("x", [P, NODE_COLS, F])
        early = sb("early", [P, 3 * NODE_COLS * F])
        h = early[:, 0:NODE_COLS * F].rearrange("p (t f) -> p t f", f=F)
        y = early[:, NODE_COLS * F:2 * NODE_COLS * F].rearrange("p (t f) -> p t f", f=F)
        agg = early[:, 2 * NODE_COLS * F:].rearrange("p (t f) -> p t f", f=F)
        dst_i = early[:, 0:ROW].bitcast(i32)
        prev_i = early[:, ROW:2 * ROW].bitcast(i32)
        type_i = early[:, 2 * ROW:3 * ROW].bitcast(i32)
        keep_b = early[:, 3 * ROW:3 * ROW + ROW // 2].bitcast(bf16)
        type_b = early[:, 3 * ROW + ROW // 2:4 * ROW].bitcast(bf16)
        sel_f = early[:, 4 * ROW:4 * ROW + 2 * KCH * P].rearrange("p (k n) -> p k n", n=P)
        head = sb("head", [P, 1], i32)
        step_98 = sb("step_98", [P, P])
        minus_col = sb("minus_col", [P, NODE_COLS + 1])
        head_f = sb("head_f", [P, 1])
        head_col = sb("head_col", [P, NODE_COLS + 1])
        node_less = sb("node_less", [P, NODE_COLS + 1])
        rows_below = sb("rows_below", [P, NODE_COLS + 1])
        inside = sb("inside", [P, 2, NODE_COLS + 1])
        first = sb("first", [P, NODE_COLS + 1])
        last = sb("last", [P, NODE_COLS])
        last_i = sb("last_i", [P, NODE_COLS], i32)
        has = sb("has", [P, NODE_COLS])
        no_edge = sb("no_edge", [P, NODE_COLS])
        place = sb("place", [P, NODE_COLS])
        past = sb("past", [P, NODE_COLS])
        place_i = sb("place_i", [P, NODE_COLS], i32)
        crosses = sb("crosses", [P, STREAMS, NODE_COLS])
        crosses2 = sb("crosses2", [P, STREAMS, NODE_COLS])
        no_cross = sb("no_cross", [P, STREAMS, NODE_COLS])
        border = sb("border", [P, STREAMS, F])
        heads4 = sb("heads4", [STREAMS, 1], i32)
        rows4 = sb("rows4", [STREAMS, F])
        node_a = sb("node_a", [P, CHUNK, F])
        node_b = sb("node_b", [P, CHUNK, F])
        node_c = sb("node_c", [P, CHUNK, F])
        stat_a = sb("stat_a", [P, CHUNK])
        stat_b = sb("stat_b", [P, CHUNK])
        stat_c = sb("stat_c", [P, CHUNK])
        last_rows = sb("last_rows", [P, 2, CHUNK, 2 * F])

        src_idx = sb("src_idx", [P, PRE, SLOTS], i32)
        xg = sb("xg", [P, 2, SLOTS, 4 * F])
        xg0 = xg[:, :, :, :].rearrange("p a k (b f) -> p (a k b f)", f=F).rearrange(
            "p (u k f) -> p u k f", u=PRE, f=F)
        ea = sb("ea", [P, 2, LEN])
        sp_in = sb("sp_in", [P, 2, SLOTS, F])
        keep = sb("keep", [P, 4, LEN], bf16)
        fresh = sb("fresh", [P, 2, LEN], bf16)
        xt = sb("xt", [P, 2, LEN])
        dt_ = sb("dt_", [P, 2, LEN])
        hid = sb("hid", [P, 2, 2, LEN])
        scan = sb("scan", [P, 2, LEN])
        out0 = sb("out0", [P, 2, SLOTS, F])
        late = sb("late", [P, LATE])
        at = [0]

        def part(n):
            at[0] += n
            return late[:, at[0] - n:at[0]]
        x4 = part(2 * STREAMS * LEN).rearrange("p (u g n) -> p u g n", u=2, g=STREAMS)
        prod = part(G_BUFS * LEN).rearrange("p (b n) -> p b n", b=G_BUFS)
        types = part(STREAMS * LEN).bitcast(bf16).rearrange("p (u g n) -> p u g n", u=2, g=STREAMS)
        onehot = part(STREAMS * LEN).bitcast(bf16).rearrange("p (u g n) -> p u g n", u=2, g=STREAMS)
        out1 = early[:, NODE_COLS * F:NODE_COLS * F + 4 * SLOTS * 2 * F].rearrange(
            "p (u k f) -> p u k f", u=4, k=SLOTS)
        at[0] = 0
        zero = part(ZERO)
        lift = part(ROW)
        lift_parts = part(ROW + 1).bitcast(bf16).rearrange("p (c n) -> p c n", c=2)
        below = part((NODE_COLS + 1) * P // 2).bitcast(bf16).rearrange("p (t n) -> p t n", n=P)
        counted = part(ROW).bitcast(bf16).rearrange("p (u n) -> p u n", u=2)
        block_i = part(ROW).bitcast(i32)
        comp = sb("comp", [P, 2, 2, LEN], bf16)
        query, score, wmsg = (hid[:, k // 2, k % 2, :] for k in range(3))
        weight = xt
        node_t = hid[:, 1, 1, :]

        psum = ctx.enter_context(nc.psum_tensor("psum", [P, 8, 512], fp32))
        bank = [psum[:, i, :] for i in range(8)]

        loaded = sem("loaded")
        heads_in = sem("heads_in")
        search_in = sem("search_in")
        edges_in = sem("edges_in")
        filled = sem("filled")
        zeroed = sem("zeroed")
        parted = sem("parted")
        prepared = sem("prepared")
        prep_out = sem("prep_out")
        lifted = sem("lifted")
        below_ready = sem("below_ready")
        fetched = [sem(f"fetched{u}") for u in range(2)]
        dve_counted = sem("dve_counted")
        act_counted = sem("act_counted")
        rows_read = sem("rows_read")
        placed = sem("placed")
        x_spread = sem("x_spread")
        ends_in = sem("ends_in")
        ends_out = sem("ends_out")
        dve_done = sem("dve_done")
        rows_got = [[sem(f"rows_got{n}_{c}") for c in range(CHUNKS)] for n in range(2)]
        border_in = [sem(f"border_in{n}") for n in range(2)]
        centred = sem("centred")
        squared = sem("squared")
        var_ready = sem("var_ready")
        dev_ready = sem("dev_ready")
        node_ready = sem("node_ready")
        turned = sem("turned")
        turned_sb = sem("turned_sb")
        mapped = sem("mapped")
        y_ready = sem("y_ready")
        picked = sem("picked")
        added = sem("added")
        h_out = sem("h_out")
        y_out = sem("y_out")
        y_spread = sem("y_spread")
        result_out = sem("result_out")

        idx_in = [[sem(f"idx_in{n}_{u}") for u in range((PRE, 2)[n])] for n in range(2)]
        ea_in = [sem(f"ea_in{u}") for u in range(2)]
        types_in = [sem(f"types_in{u}") for u in range(2)]
        spread_in = [[sem(f"spread_in{n}_{u}") for u in range(2)] for n in range(2)]
        keep_in = [[sem(f"keep_in{n}_{u}") for u in range(4)] for n in range(2)]
        gathered = [[sem(f"gathered{n}_{u}") for u in range((PRE, 2)[n])] for n in range(2)]
        stored = [[sem(f"stored{n}_{u}") for u in range((2, 4)[n])] for n in range(2)]
        x_turned = [sem(f"x_turned{n}") for n in range(2)]
        x_ready = [sem(f"x_ready{n}") for n in range(2)]
        s_turned = [sem(f"s_turned{n}") for n in range(2)]
        d_ready = [sem(f"d_ready{n}") for n in range(2)]
        scanned = [sem(f"scanned{n}") for n in range(2)]
        o_turned = [sem(f"o_turned{n}") for n in range(2)]
        o_ready = [sem(f"o_ready{n}") for n in range(2)]
        fresh_ready = sem("fresh_ready")
        hid_done = sem("hid_done")
        relu_done = sem("relu_done")
        v_done = sem("v_done")
        onehot_ready = sem("onehot_ready")
        comp_done = sem("comp_done")
        comp_ready = sem("comp_ready")
        rel_done = sem("rel_done")
        key_done = sem("key_done")
        query_ready = sem("query_ready")
        score_ready = sem("score_ready")
        sum_done = sem("sum_done")
        weight_ready = sem("weight_ready")
        coef_done = sem("coef_done")
        prod_ready = sem("prod_ready")
        msg_done = sem("msg_done")
        wmsg_ready = sem("wmsg_ready")
        src_copied = sem("src_copied")

        waits_passed = {nc.sync: sem("sp_passed"), nc.gpsimd: sem("pool_passed")}
        N_CONST = 16
        N_SEARCH = 8
        block = ctx.enter_context(nc.Block())

        def wait_count(eng, s, semaphore, count):
            if s.known and count <= 0:
                return
            eng.wait_ge(semaphore, count)
            if not s.known and eng in waits_passed:
                eng.sem_inc(waits_passed[eng], 1)

        def wait_in(eng, s, semaphores, each=16):
            wait_count(eng, s, semaphores[s.slot(len(semaphores))], (s.earlier(len(semaphores)) + 1) * each)

        def wait_out(eng, s, semaphores, each=16):
            wait_count(eng, s, semaphores[s.slot(len(semaphores))], s.earlier(len(semaphores)) * each)

        def wait_step(eng, s, semaphore, each=1, lag=0, more=0):
            wait_count(eng, s, semaphore, (s.at - lag + 1) * each + more)

        found = [psum[:, 4 * u:4 * u + 4, :].rearrange("p b n -> p (b n)")[:, 0:ROW] for u in range(2)]
        rows_found = [psum[:, 4 * u + 3, 256:256 + NODE_COLS + 1] for u in range(2)]

        spread_v = spread[0:EDGES, :].rearrange("(s p k) f -> s p k f", s=STEPS, p=P)
        spread_heads = spread[0:STREAMS, :]
        max_v = max_rows.rearrange("(s p k) f -> s p k f", s=STEPS, p=P)
        sum_v = sum_rows.rearrange("(s p k) f -> s p k f", s=STEPS, p=P)
        keep_v = keep_dram.rearrange("(g s n) -> s g n", g=STREAMS, s=STEPS)
        type_v = type_dram.rearrange("(g s n) -> s g n", g=STREAMS, s=STEPS)
        ea_v = t["edge_t"].rearrange("p (s n) -> s p n", s=STEPS)
        idx_v = t["src_t"]
        h_nodes = h_dram.rearrange("(p t) (c f) -> p t c f", p=P, f=F)
        y_nodes = y_dram.rearrange("(p t) f -> p t f", p=P)
        full = N_NODES // NODE_COLS
        tail = N_NODES - full * NODE_COLS
        out_full = t["out"][0:full * NODE_COLS, :].rearrange("(p t) f -> p t f", p=full)
        out_tail = t["out"][full * NODE_COLS:, :].rearrange("(p t) f -> p t f", p=1)

        def border_rows(eng, table, n):
            ends = table[EDGES - STREAMS:EDGES, 0:F]
            eng.dma_start(border[:, :, :], ends.partition_broadcast(P)).then_inc(border_in[n], 16)

        @block.sync
        def _(sp):
            def index_load0(s):
                wait_out(sp, s, gathered[0], 16 * SLOTS)
                sp.dma_start(src_idx[:, s.slot(PRE), :], idx_v[s.at]).then_inc(idx_in[0][s.slot(PRE)], 16)

            for off in range(PRE):
                index_load0(Step(PRE, 0, off))
            sp.dma_start(heads4[:, :], t["heads4"]).then_inc(heads_in, 16)
            sp.dma_start(dst_i, t["dst_rows"]).then_inc(search_in, 16)
            sp.dma_start(block_i, t["block_rows"]).then_inc(search_in, 16)
            for tile, name in ((head, "head"), (step_98, "step_98"), (minus_col, "minus_col"),
                               (node_less, "node_less"), (node_half, "node_half"),
                               (spare_id, "spare_id")):
                sp.dma_start(tile[:, :], t[name]).then_inc(search_in, 16)
            sp.dma_start(prev_i, t["prev_rows"]).then_inc(edges_in, 16)
            sp.dma_start(type_i, t["type_rows"]).then_inc(edges_in, 16)
            for tile, name in ((row_id, "row_id"),
                               (ident, "ident"), (w1, "w1"), (w2, "w2"), (b1, "b1"), (a1w, "a1w"),
                               (a1b, "a1b"), (a2w, "a2w"), (self_w, "self_w"), (basis, "basis"),
                               (ones_blk, "ones_blk"), (sel_f, "sel"), (x, "x_nodes")):
                every = tuple(slice(None) for _ in tile.shape)
                sp.dma_start(tile[every], t[name]).then_inc(loaded, 16)
            sp.dma_start(b2[:, :], t["b2"].partition_broadcast(P)).then_inc(loaded, 16)
            sp.dma_start(a2b[:, :], t["a2b"].partition_broadcast(P)).then_inc(loaded, 16)
            sp.dma_start(rel[:, :], t["rel"]).then_inc(loaded, 16)
            sp.wait_ge(prepared, 2)
            sp.dma_start(keep_dram.rearrange("(p n) -> p n", p=P), keep_b).then_inc(prep_out, 16)
            sp.dma_start(type_dram.rearrange("(p n) -> p n", p=P), type_b).then_inc(prep_out, 16)
            sp.wait_ge(prep_out, 32)
            sp.wait_ge(ends_in, 16)
            sp.wait_ge(zeroed, 16 * N_ZERO)
            sp.dma_start(spread_heads, rows4[:, :]).then_inc(ends_out, 16)
            sp.wait_ge(x_spread, 16 * NODE_COLS)

            def keep_load(n, s):
                wait_step(sp, s, scanned[n], lag=4)
                for g in range(STREAMS):
                    sp.dma_start(keep[F * g:F * g + F, s.slot(4), :],
                                 keep_v[s.at][g].partition_broadcast(F)).then_inc(keep_in[n][s.slot(4)], 16)

            def loads0(s):
                index = s.plus(PRE - 2)
                if index.exists() and (not s.known or index.at >= PRE):
                    index_load0(index)
                wait_step(sp, s, s_turned[0], lag=2)
                sp.dma_start(sp_in[:, s.slot(2)], spread_v[s.at]).then_inc(spread_in[0][s.slot(2)], 16)
                wait_step(sp, s, hid_done, each=2, lag=2)
                sp.dma_start(ea[:, s.slot(2), :], ea_v[s.at]).then_inc(ea_in[s.slot(2)], 16)
                keep_load(0, s)

            run_steps(sp, loads0, PRE)

            for u in range(2):
                sp.wait_ge(stored[0][u], 16 * (STEPS // 2))
            border_rows(sp, max_rows, 0)
            for c in range(CHUNKS):
                cols = slice(c * CHUNK, (c + 1) * CHUNK)
                sp.wait_ge(node_ready, c + 1)
                for k in range(4):
                    sp.dma_start(h_nodes[:, cols, k, :], h[:, cols, :]).then_inc(h_out, 16)
                sp.wait_ge(y_ready, c + 1)
                sp.dma_start(y_nodes[:, cols, :], y[:, cols, :]).then_inc(y_out, 16)
            sp.wait_ge(ends_in, 32)
            sp.wait_ge(y_spread, 16 * NODE_COLS)
            sp.dma_start(spread_heads, rows4[:, :]).then_inc(ends_out, 16)
            sp.wait_ge(ends_out, 32)

            def loads1(s):
                wait_out(sp, s, gathered[1], 16 * SLOTS)
                sp.dma_start(src_idx[:, s.slot(2), :], idx_v[s.at]).then_inc(idx_in[1][s.slot(2)], 16)
                wait_step(sp, s, onehot_ready, lag=2)
                sp.dma_start(types[:, s.slot(2)], type_v[s.at].partition_broadcast(P)
                             ).then_inc(types_in[s.slot(2)], 16)
                wait_step(sp, s, s_turned[1], lag=2)
                sp.dma_start(sp_in[:, s.slot(2)], spread_v[s.at]).then_inc(spread_in[1][s.slot(2)], 16)
                keep_load(1, s)

            run_steps(sp, loads1, 4)

            for u in range(4):
                sp.wait_ge(stored[1][u], 16 * (STEPS // 4))
            border_rows(sp, sum_rows, 1)
            for c in range(CHUNKS):
                cols = slice(c * CHUNK, (c + 1) * CHUNK)
                sp.wait_ge(node_ready, CHUNKS + c + 1)
                sp.dma_start(out_full[:, cols, :], agg[0:full, cols, :]).then_inc(result_out, 16)
                got = min((c + 1) * CHUNK, tail) - c * CHUNK
                if got > 0:
                    cols = slice(c * CHUNK, c * CHUNK + got)
                    sp.dma_start(out_tail[:, cols, :], agg[full:full + 1, cols, :]).then_inc(result_out, 16)
            sp.wait_ge(result_out, 16 * (CHUNKS + -(-tail // CHUNK)))

        @block.gpsimd
        def _(pool):
            def gather(out, table, index, done):
                pool.indirect_dma_start(out=out, out_offset=None, in_=table,
                                        in_offset=bass.IndirectOffsetOnAxis(ap=index, axis=0)).then_inc(done, 16)

            def scatter(table, index, rows_, done):
                pool.indirect_dma_start(out=table, out_offset=bass.IndirectOffsetOnAxis(ap=index, axis=0),
                                        in_=rows_, in_offset=None).then_inc(done, 16)

            def gathers0(s):
                wait_in(pool, s, idx_in[0])
                wait_step(pool, s, x_turned[0], lag=PRE)
                for k in range(SLOTS):
                    gather(xg0[:, s.slot(PRE), k, :], t["x_dram"], src_idx[:, s.slot(PRE), k:k + 1],
                           gathered[0][s.slot(PRE)])

            for off in range(PRE):
                gathers0(Step(PRE, 0, off))
            pool.wait_ge(heads_in, 16)
            gather(rows4[:, :], t["x_dram"], heads4[:, :], ends_in)
            pool.wait_ge(loaded, 16 * N_CONST)
            pool.wait_ge(zeroed, 16 * N_ZERO)
            pool.wait_ge(ends_out, 16)
            for k in range(NODE_COLS):
                if k in (0, EARLY_COLS):
                    pool.wait_ge(placed, 1 + (k > 0))
                scatter(spread, place_i[:, k:k + 1], x[:, k, :], x_spread)

            with pool.Fori(1, STEPS // PRE) as i:
                for off in range(PRE):
                    gathers0(Step(PRE, i, off))

            for u in range(2):
                pool.wait_ge(stored[0][u], 16 * (STEPS // 2))
            for c in range(CHUNKS):
                for k in range(c * CHUNK, (c + 1) * CHUNK):
                    gather(agg[:, k, :], max_rows, last_i[:, k:k + 1], rows_got[0][c])
            for c in range(CHUNKS):
                pool.wait_ge(y_ready, c + 1)
                for k in range(c * CHUNK, (c + 1) * CHUNK):
                    scatter(spread, place_i[:, k:k + 1], y[:, k, :], y_spread)
            pool.wait_ge(y_out, 16 * CHUNKS)
            gather(rows4[:, :], y_dram, heads4[:, :], ends_in)
            pool.wait_ge(h_out, 4 * 16 * CHUNKS)

            def gathers1(s):
                wait_in(pool, s, idx_in[1])
                wait_step(pool, s, x_turned[1], each=STREAMS, lag=2)
                wait_step(pool, s, src_copied, lag=2)
                for k in range(SLOTS):
                    gather(xg[:, s.slot(2), k, :], h_dram, src_idx[:, s.slot(2), k:k + 1],
                           gathered[1][s.slot(2)])

            run_steps(pool, gathers1, 4)

            for u in range(4):
                pool.wait_ge(stored[1][u], 16 * (STEPS // 4))
            for c in range(CHUNKS):
                if c >= 2:
                    pool.wait_ge(added, c - 1)
                    pool.wait_ge(picked, c - 1)
                for k in range(CHUNK):
                    col = c * CHUNK + k
                    gather(last_rows[:, c % 2, k, :], sum_rows, last_i[:, col:col + 1], rows_got[1][c])

        @block.scalar
        def _(act):
            act.wait_ge(filled, 1)
            act.wait_ge(search_in, 16 * N_SEARCH)
            flat = spread[0:EDGES, :].rearrange("e f -> (e f)").rearrange("(k p n) -> k p n", p=P, n=ZERO)
            for k in range(N_ZERO):
                act.dma_start(flat[k], zero).then_inc(zeroed, 16)
            for k in range(1, NODE_COLS + 1, 2):
                for q, (a, b) in enumerate(HALVES):
                    act.wait_ge(fetched[1], 2 * (k // 2) + q + 1)
                    if k > 1:
                        act.wait_ge(act_counted, 2 * (k // 2) + q - 1)
                    act.activation(counted[:, 1, a:b], found[1][:, a:b], ACT.Sign, bias=node_half[:, k:k + 1],
                                   scale=-1.0, accum_out=inside[:, q, k:k + 1]).then_inc(act_counted, 1)
            act.wait_ge(loaded, 16 * N_CONST)

            def store(n, s, tile, view):
                wait_step(act, s, o_ready[n])
                act.dma_start(view[s.at], tile).then_inc(stored[n][s.slot(len(stored[n]))], 16)

            def step0(s):
                u = s.slot(2)
                wait_step(act, s, x_turned[0])
                wait_step(act, s, hid_done, each=2, lag=2)
                act.copy(xt[:, u, :], bank[0][:, :]).then_inc(x_ready[0], 1)
                for q in range(2):
                    wait_step(act, s, hid_done, each=2, more=q - 1)
                    wait_step(act, s, v_done, lag=2)
                    act.activation(hid[:, u, q, :], bank[2 + q][:, :], ACT.Relu,
                                   bias=b1[:, 0:1]).then_inc(relu_done, 1)
                wait_step(act, s, o_turned[0])
                wait_out(act, s, stored[0])
                act.copy(out0[:, u].rearrange("p k f -> p (k f)"), bank[5][:, :]).then_inc(o_ready[0], 1)
                store(0, s, out0[:, u], max_v)

            run_steps(act, step0, PRE)

            def layer_norm(n):
                act.wait_ge(centred, n + 1)
                act.activation(node_c[:, :, :], node_b[:, :, :], ACT.Square).then_inc(squared, 1)
                act.wait_ge(var_ready, n + 1)
                act.activation(stat_b[:, :], stat_a[:, :], ACT.Sqrt, bias=eps[:, 0:1],
                               scale=1.0 / F).then_inc(dev_ready, 1)

            def turned_copy(n):
                act.wait_ge(turned, n + 1)
                if n > 0:
                    act.wait_ge(mapped, n)
                whole = P * sum(b - a == 4 for a, b in GROUPS)
                rest_rows = F * (CHUNK % 4)
                act.copy(node_t[:, 0:whole], bank[6][:, 0:whole])
                act.copy(node_t[0:rest_rows, whole:whole + P],
                         bank[6][0:rest_rows, whole:whole + P]).then_inc(turned_sb, 1)

            for c in range(CHUNKS):
                layer_norm(c)
                turned_copy(c)

            def comp_copies(s):
                for q in range(2):
                    wait_step(act, s, comp_done)
                    wait_step(act, s, coef_done, each=SLOTS, lag=2)
                    act.copy(comp[:, s.slot(2), q, :], bank[q][:, :]).then_inc(comp_ready, 1)

            def x4_copy(s, g):
                wait_step(act, s, x_turned[1], each=STREAMS, more=g - 3)
                wait_step(act, s, prod_ready, each=SLOTS, lag=2)
                wait_step(act, s, key_done, lag=2)
                act.copy(x4[:, s.slot(2), g, :], bank[g % 2][:, :]).then_inc(x_ready[1], 1)

            def attend(s):
                wait_step(act, s, sum_done)
                wait_step(act, s, wmsg_ready, lag=2)
                act.activation(weight[:, s.slot(2), :], bank[1][:, :], ACT.Tanh, scale=float(F) ** -0.5
                               ).then_inc(weight_ready, 1)

            def src_copy(s):
                wait_in(act, s, gathered[1], 16 * SLOTS)
                wait_out(act, s, stored[1])
                act.copy(out1[:, s.slot(4), :, F:2 * F], xg[:, s.slot(2), :, 0:F]).then_inc(src_copied, 1)

            def finish(s):
                wait_step(act, s, o_turned[1])
                act.copy(out1[:, s.slot(4), :, 0:F], bank[4][:, :].rearrange("p (k f) -> p k f", f=F)
                         ).then_inc(o_ready[1], 1)
                wait_step(act, s, src_copied)
                store(1, s, out1[:, s.slot(4)], sum_v)

            def step1(s):
                ahead, behind = s.plus(1), s.plus(-1)
                attend(s)
                if ahead.exists():
                    comp_copies(ahead)
                    for g in range(STREAMS):
                        x4_copy(ahead, g)
                    src_copy(ahead)
                if behind.exists():
                    finish(behind)

            comp_copies(Step(4, 0, 0))
            for g in range(STREAMS):
                x4_copy(Step(4, 0, 0), g)
            src_copy(Step(4, 0, 0))
            run_steps(act, step1, 4)
            finish(Step(4, 0, STEPS - 1))

            for c in range(CHUNKS):
                act.wait_ge(rows_got[1][c], 16 * CHUNK)
                if c > 0:
                    act.wait_ge(turned, CHUNKS + c)
                act.copy(y[:, 0:CHUNK, :], last_rows[:, c % 2, :, F:2 * F]).then_inc(picked, 1)
                turned_copy(CHUNKS + c)
                layer_norm(CHUNKS + c)

        @block.vector
        def _(dve):
            done = [0]

            def link(ins):
                done[0] += 1
                ins.then_inc(dve_done, 1)
                dve.wait_ge(dve_done, done[0])

            dve.memset(zero, 0.0).then_inc(filled, 1)
            link(dve.memset(eps[:, :], EPS))
            link(dve.memset(comp_lhs[:, :], 0.0))
            dve.wait_ge(search_in, 16 * N_SEARCH)
            link(dve.tensor_tensor(lift, dst_i, block_i, ALU.subtract))
            link(dve.tensor_copy(lift_parts[:, 0, 0:ROW], lift))
            dve.tensor_tensor(lift_parts[:, 1, 0:ROW], lift, lift_parts[:, 0, 0:ROW], ALU.subtract
                              ).then_inc(lifted, 1)
            dve.memset(lift_parts[:, 0, ROW:ROW + 1], 1.0).then_inc(lifted, 1)
            link(dve.tensor_copy(head_f[:, :], head[:, :]))
            link(dve.tensor_scalar(head_col[:, :], minus_col[:, :], head_f[:, 0:1], None, ALU.add))

            def count(k):
                for q, (a, b) in enumerate(HALVES):
                    dve.wait_ge(fetched[0], 2 * (k // 2) + q + 1)
                    if k > 0:
                        dve.wait_ge(dve_counted, 2 * (k // 2) + q - 1)
                    dve.tensor_scalar(counted[:, 0, a:b], found[0][:, a:b], node_less[:, k:k + 1], None,
                                      ALU.is_lt, ALU.add, accum_out=inside[:, q, k:k + 1]
                                      ).then_inc(dve_counted, 1)

            def table_row(edge, out, a, b):
                link(dve.tensor_scalar(out, edge, float(STREAMS), None, ALU.mult))
                for g in range(1, STREAMS):
                    link(dve.tensor_scalar(past[:, a:b], edge, float(g * STREAM), float(1 - EDGES), ALU.is_ge,
                                           ALU.mult))
                    link(dve.tensor_tensor(out, out, past[:, a:b], ALU.add))

            def place_nodes(a, b):
                lo = a + 1 if a > 0 else 0
                for semaphore in (dve_counted, fetched[0]):
                    dve.wait_ge(semaphore, 2 * ((b + 2) // 2))
                for semaphore in (act_counted, fetched[1]):
                    dve.wait_ge(semaphore, 2 * ((b + 1) // 2))
                even, odd = (slice(lo + (u - lo) % 2, b + 1, 2) for u in range(2))
                new = slice(lo, b + 1)
                for u, cols in enumerate((even, odd)):
                    dve.tensor_scalar(rows_below[:, cols], rows_found[u][:, cols], -1.0, 0.0, ALU.add,
                                      ALU.max).then_inc(rows_read, 1)
                link(dve.tensor_tensor(inside[:, 0, new], inside[:, 0, new], inside[:, 1, new], ALU.add))
                link(dve.tensor_scalar(inside[:, 0, odd], inside[:, 0, odd], 0.5, 0.5 * ROW, ALU.mult, ALU.add))
                dve.wait_ge(rows_read, 2 if a == 0 else 4)
                link(dve.scalar_tensor_tensor(first[:, new], rows_below[:, new], float(ROW), inside[:, 0, new],
                                              ALU.mult, ALU.add))
                begin, end = first[:, a:b], first[:, a + 1:b + 1]
                row, spare = place[:, a:b], spare_id[:, a:b]
                link(dve.tensor_tensor(has[:, a:b], end, begin, ALU.is_gt))
                table_row(begin, row, a, b)
                link(dve.tensor_tensor(row, row, spare, ALU.subtract))
                link(dve.tensor_tensor(row, row, has[:, a:b], ALU.mult))
                link(dve.tensor_tensor(row, row, spare, ALU.add))
                dve.tensor_copy(place_i[:, a:b], row).then_inc(placed, 1)

            next_count = 0
            for c in range(SEARCHES):
                cols = slice(c * SEARCH, (c + 1) * SEARCH)
                dve.tensor_tensor(below[:, cols, :], bc(step_98[:, :], [P, SEARCH, P], 1),
                                  bc(head_col[:, cols], [P, SEARCH, P], 2), ALU.is_gt).then_inc(below_ready, 1)
                if c == 1:
                    dve.wait_ge(edges_in, 32)
                    dve.tensor_tensor(keep_b, dst_i, prev_i, ALU.is_equal).then_inc(prepared, 1)
                    dve.tensor_copy(type_b, type_i).then_inc(prepared, 1)
                while next_count < c * SEARCH:
                    count(next_count)
                    next_count += 2
                if c * SEARCH == EARLY_COLS + 1:
                    place_nodes(0, EARLY_COLS)
            while next_count < NODE_COLS + 1:
                count(next_count)
                next_count += 2
            place_nodes(EARLY_COLS, NODE_COLS)
            dve.wait_ge(placed, 2)
            begin, end = first[:, 0:NODE_COLS], first[:, 1:NODE_COLS + 1]
            link(dve.tensor_scalar(last[:, :], end, -1.0, 0.0, ALU.add, ALU.max))
            table_row(last[:, :], place[:, :], 0, NODE_COLS)
            link(dve.tensor_copy(last_i[:, :], place[:, :]))
            link(dve.tensor_scalar(no_edge[:, :], has[:, :], -1.0, BIG, ALU.add, ALU.mult))
            for g in range(1, STREAMS):
                link(dve.tensor_scalar(crosses2[:, g, :], begin, float(g * STREAM), None, ALU.is_lt))
                link(dve.tensor_scalar(crosses[:, g, :], last[:, :], float(g * STREAM), None, ALU.is_ge))
                link(dve.tensor_tensor(crosses[:, g, :], crosses[:, g, :], crosses2[:, g, :], ALU.mult))
                link(dve.tensor_scalar(no_cross[:, g, :], crosses[:, g, :], -1.0, BIG, ALU.add, ALU.mult))

            dve.wait_ge(loaded, 16 * N_CONST)
            link(dve.tensor_copy(rel_parts[:, 0, :], rel[:, :]))
            link(dve.tensor_tensor(rest[:, :], rel[:, :], rel_parts[:, 0, :], ALU.subtract))
            link(dve.tensor_copy(rel_parts[:, 1, :], rest[:, :]))
            link(dve.tensor_tensor(rest2[:, :], rest[:, :], rel_parts[:, 1, :], ALU.subtract))
            link(dve.tensor_copy(rel_parts[:, 2, :], rest2[:, :]))
            for q in range(PARTS):
                link(dve.tensor_copy(comp_lhs[:, q * BASES:(q + 1) * BASES], rel_parts[:, q, F:F + BASES]))
            dve.tensor_copy(sel[:, :, :], sel_f[:, :, :]).then_inc(parted, 1)

            def before(s, tile, start=0.0):
                u = s.slot(2)
                return start if s.known and s.at == 0 else tile[:, 1 - u, LEN - 1:LEN]

            def spread_scan(n, s, b):
                wait_in(dve, s, keep_in[n], 16 * STREAMS)
                wait_step(dve, s, s_turned[n])
                wait_step(dve, s, d_ready[n], lag=1)
                dve.tensor_tensor_scan(dt_[:, s.slot(2), :], keep[:, s.slot(4), :], bank[b][:, :],
                                       before(s, dt_), ALU.mult, ALU.add).then_inc(d_ready[n], 1)

            def step0(s):
                u = s.slot(2)
                wait_step(dve, s, hid_done, each=2, lag=2)
                spread_scan(0, s, 1)
                wait_step(dve, s, scanned[0], lag=2)
                dve.tensor_scalar(fresh[:, u, :], keep[:, s.slot(4), :], -1.0, BIG, ALU.add, ALU.mult
                                  ).then_inc(fresh_ready, 1)
                wait_step(dve, s, v_done)
                wait_step(dve, s, fresh_ready)
                wait_step(dve, s, o_turned[0], lag=2)
                wait_step(dve, s, scanned[0], lag=1)
                dve.tensor_tensor_scan(scan[:, u, :], fresh[:, u, :], bank[4][:, :], before(s, scan, -BIG),
                                       ALU.add, ALU.max).then_inc(scanned[0], 1)

            run_steps(dve, step0, PRE)

            shape = [P, CHUNK, F]

            def layer_norm(n, out):
                link(dve.tensor_reduce(stat_a[:, :], node_a[:, :, :], AX.X, ALU.add))
                link(dve.tensor_scalar(stat_c[:, :], stat_a[:, :], 1.0 / F, None, ALU.mult))
                dve.tensor_tensor(node_b[:, :, :], node_a[:, :, :], bc(stat_c[:, :], shape, 2), ALU.subtract
                                  ).then_inc(centred, 1)
                dve.wait_ge(centred, n + 1)
                dve.wait_ge(squared, n + 1)
                dve.tensor_reduce(stat_a[:, :], node_c[:, :, :], AX.X, ALU.add).then_inc(var_ready, 1)
                dve.wait_ge(dev_ready, n + 1)
                link(dve.reciprocal(stat_c[:, :], stat_b[:, :]))
                dve.tensor_tensor(out, node_b[:, :, :], bc(stat_c[:, :], shape, 2), ALU.mult
                                  ).then_inc(node_ready, 1)
                dve.wait_ge(node_ready, n + 1)

            dve.wait_ge(border_in[0], 16)
            for c in range(CHUNKS):
                cols = slice(c * CHUNK, (c + 1) * CHUNK)
                dve.wait_ge(rows_got[0][c], 16 * CHUNK)
                v = agg[:, cols, :]
                for g in range(1, STREAMS):
                    link(dve.tensor_tensor(node_b[:, :, :], bc(border[:, g - 1, :], shape, 1),
                                           bc(no_cross[:, g, cols], shape, 2), ALU.add))
                    link(dve.tensor_tensor(v, v, node_b[:, :, :], ALU.max))
                link(dve.tensor_tensor(v, v, bc(b2[:, :], shape, 1), ALU.add))
                link(dve.tensor_tensor(v, v, bc(no_edge[:, cols], shape, 2), ALU.add))
                link(dve.tensor_tensor(v, v, x[:, cols, :], ALU.max))
                link(dve.tensor_tensor(node_a[:, :, :], v, x[:, cols, :], ALU.add))
                layer_norm(c, h[:, cols, :])
                dve.wait_ge(mapped, c + 1)
                dve.tensor_tensor(y[:, cols, :], bank[7][:, 0:CHUNK * F].rearrange("p (t f) -> p t f", f=F),
                                  bc(a2b[:, :], shape, 1), ALU.add).then_inc(y_ready, 1)

            def one_hot(s):
                wait_in(dve, s, types_in)
                wait_step(dve, s, rel_done, lag=2)
                dve.tensor_scalar(onehot[:, s.slot(2), :, :], types[:, s.slot(2), :, :], row_id[:, 0:1], None,
                                  ALU.is_equal).then_inc(onehot_ready, 1)

            def find_query(s):
                wait_step(dve, s, d_ready[1])
                wait_step(dve, s, rel_done)
                wait_step(dve, s, score_ready, lag=1)
                dve.tensor_tensor(query, dt_[:, s.slot(2), :], bank[5][:, :], ALU.add).then_inc(query_ready, 1)

            def find_score(s):
                wait_step(dve, s, query_ready)
                wait_step(dve, s, key_done)
                wait_step(dve, s, sum_done, lag=1)
                dve.scalar_tensor_tensor(score, bank[0][:, :], a1b[:, 0:1], query, ALU.add, ALU.mult
                                         ).then_inc(score_ready, 1)

            def product(s, n):
                k, g = divmod(n, STREAMS)
                wait_step(dve, s, coef_done, each=SLOTS, more=n - SLOTS + 1)
                wait_step(dve, s, x_ready[1], each=STREAMS, more=g - 3)
                wait_step(dve, s, msg_done, each=KCH, more=k - 3 - G_BUFS // STREAMS)
                dve.tensor_tensor(prod[:, n % G_BUFS, :], x4[:, s.slot(2), g, :],
                                  bank[C_BANK[n]][:, :], ALU.mult).then_inc(prod_ready, 1)

            def weigh(s):
                wait_step(dve, s, msg_done, each=KCH)
                wait_step(dve, s, weight_ready)
                wait_step(dve, s, scanned[1], lag=1)
                dve.scalar_tensor_tensor(wmsg, weight[:, s.slot(2), :], 0.0, bank[7][:, :], ALU.max, ALU.mult
                                         ).then_inc(wmsg_ready, 1)

            def sum_scan(s):
                wait_step(dve, s, wmsg_ready)
                wait_step(dve, s, o_turned[1], lag=2)
                dve.tensor_tensor_scan(scan[:, s.slot(2), :], keep[:, s.slot(4), :], wmsg, before(s, scan),
                                       ALU.mult, ALU.add).then_inc(scanned[1], 1)

            def step1(s):
                for n in range(SLOTS):
                    product(s, n)
                    if n == 3 and s.plus(-1).exists():
                        weigh(s.plus(-1))
                    if n == 4 and s.plus(-1).exists():
                        sum_scan(s.plus(-1))
                    if n == 5 and s.plus(2).exists():
                        one_hot(s.plus(2))
                    if n == 7 and s.plus(1).exists():
                        spread_scan(1, s.plus(1), 4)
                    if n == 8 and s.plus(1).exists():
                        find_query(s.plus(1))
                    if n == (15 if s.known and s.at == STEPS - 2 else 13) and s.plus(1).exists():
                        find_score(s.plus(1))

            first_step = Step(4, 0, 0)
            one_hot(first_step)
            one_hot(first_step.plus(1))
            spread_scan(1, first_step, 4)
            find_query(first_step)
            find_score(first_step)
            run_steps(dve, step1, 4)
            weigh(Step(4, 0, STEPS - 1))
            sum_scan(Step(4, 0, STEPS - 1))

            dve.wait_ge(border_in[1], 16)
            for c in range(CHUNKS):
                cols = slice(c * CHUNK, (c + 1) * CHUNK)
                dve.wait_ge(rows_got[1][c], 16 * CHUNK)
                v = agg[:, cols, :]
                nei = last_rows[:, c % 2, :, 0:F]
                for g in range(1, STREAMS):
                    link(dve.tensor_tensor(node_b[:, :, :], bc(border[:, g - 1, :], shape, 1),
                                           bc(crosses[:, g, cols], shape, 2), ALU.mult))
                    link(dve.tensor_tensor(v, nei if g == 1 else v, node_b[:, :, :], ALU.add))
                dve.wait_ge(mapped, CHUNKS + c + 1)
                dve.tensor_tensor(node_a[:, :, :], v, bank[7][:, 0:CHUNK * F].rearrange("p (t f) -> p t f", f=F),
                                  ALU.add).then_inc(added, 1)
                dve.wait_ge(added, c + 1)
                link(dve.tensor_tensor(node_b[:, :, :], node_a[:, :, :], bc(has[:, cols], shape, 2), ALU.mult))
                link(dve.scalar_tensor_tensor(node_a[:, :, :], node_b[:, :, :], 0.0, h[:, cols, :],
                                              ALU.max, ALU.add))
                layer_norm(CHUNKS + c, v)

        @block.tensor
        def _(pe):
            pe.wait_ge(lifted, 2)
            for k in range(NODE_COLS + 1):
                u = k % 2
                if k == EARLY_COLS + 1:
                    pe.wait_ge(rows_read, 2)
                if k % SEARCH == 0:
                    pe.wait_ge(below_ready, k // SEARCH + 1)
                for q, half in enumerate(HALVES):
                    if k >= 2:
                        pe.wait_ge((dve_counted, act_counted)[u], 2 * (k // 2) + q - 1)
                    for a in range(*half, 512):
                        b = min(a + 512, ROW)
                        for c in range(2):
                            last_ = pe.matmul(found[u][:, a:b], below[:, k, :], lift_parts[:, c, a:b],
                                              start=c == 0, stop=c == 1)
                    if q == 1:
                        last_ = pe.matmul(rows_found[u][:, k:k + 1], below[:, k, :],
                                          lift_parts[:, 0, ROW:ROW + 1], start=True, stop=True)
                    last_.then_inc(fetched[u], 1)
            pe.wait_ge(loaded, 16 * N_CONST)
            pe.wait_ge(parted, 1)

            def spread_turn(n, s, b):
                wait_in(pe, s, spread_in[n])
                out = bank[b][:, :].rearrange("p (n j) -> p j n", j=TILES)
                for j in range(TILES):
                    last_ = pe.transpose(out[:, j, :], sp_in[:, s.slot(2), j * STREAMS:(j + 1) * STREAMS, :],
                                         ident[:, :])
                last_.then_inc(s_turned[n], 1)

            def scan_turn(n, s, b):
                wait_step(pe, s, scanned[n])
                wait_step(pe, s, o_ready[n], lag=1)
                src = scan[:, s.slot(2), :].rearrange("p (n j) -> p j n", j=TILES)
                for j in range(TILES):
                    last_ = pe.transpose(bank[b][:, P * j:P * j + P], src[:, j, :], ident[:, :])
                last_.then_inc(o_turned[n], 1)

            def step0(s):
                u = s.slot(2)
                wait_in(pe, s, gathered[0], 16 * SLOTS)
                wait_step(pe, s, x_ready[0], lag=1)
                out = bank[0][:, :].rearrange("p (n j) -> p j n", j=TILES)
                for j in range(TILES):
                    last_ = pe.transpose(out[:, j, :], xg0[:, s.slot(PRE), j * STREAMS:(j + 1) * STREAMS, :],
                                         ident[:, :])
                last_.then_inc(x_turned[0], 1)
                wait_step(pe, s, d_ready[0], lag=1)
                spread_turn(0, s, 1)
                wait_step(pe, s, x_ready[0])
                wait_in(pe, s, ea_in)
                for q in range(2):
                    wait_step(pe, s, relu_done, each=2, lag=1, more=q - 1)
                    for k, rhs in enumerate((xt, ea, dt_)):
                        if rhs is dt_:
                            wait_step(pe, s, d_ready[0])
                        last_ = pe.matmul(bank[2 + q][:, :], w1[:, (0, 2, 1)[k], q, :], rhs[:, u, :],
                                          start=k == 0, stop=k == 2)
                    last_.then_inc(hid_done, 1)
                wait_step(pe, s, scanned[0], lag=1)
                for q in range(2):
                    wait_step(pe, s, relu_done, each=2, more=q - 1)
                    last_ = pe.matmul(bank[4][:, :], w2[:, q, :], hid[:, u, q, :], start=q == 0, stop=q == 1)
                last_.then_inc(v_done, 1)
                scan_turn(0, s, 5)

            run_steps(pe, step0, PRE)

            def node_map(n, source, weights):
                if n > 0:
                    pe.wait_ge(turned_sb, n)
                for k, (a, b) in enumerate(GROUPS):
                    m = F * (b - a)
                    last_ = pe.transpose(bank[6][0:m, P * k:P * k + P], source[:, a:b, :], ident[:, :])
                last_.then_inc(turned, 1)
                pe.wait_ge(turned_sb, n + 1)
                for k, (a, b) in enumerate(GROUPS):
                    m = F * (b - a)
                    last_ = pe.matmul(bank[7][:, F * a:F * b], node_t[0:m, P * k:P * k + P],
                                      weights[0:m, 0:m], start=True, stop=True)
                last_.then_inc(mapped, 1)

            for c in range(CHUNKS):
                pe.wait_ge(node_ready, c + 1)
                if c > 0:
                    pe.wait_ge(y_ready, c)
                node_map(c, h[:, c * CHUNK:(c + 1) * CHUNK, :], a2w)

            def coef(s, n):
                k, g = divmod(n, STREAMS)
                wait_step(pe, s, prod_ready, each=SLOTS, lag=1, more=C_FREE[n])
                pe.matmul(bank[C_BANK[n]][:, :], sel[:, (g % 2) * KCH + k, :], comp[:, s.slot(2), g // 2, :],
                          start=True, stop=True).then_inc(coef_done, 1)

            def messages(s, k):
                wait_step(pe, s, prod_ready, each=SLOTS, more=(k + 1) * STREAMS - SLOTS)
                if k == 0:
                    wait_step(pe, s, wmsg_ready, lag=1)
                for g in range(STREAMS):
                    last_ = pe.matmul(bank[7][F * g:F * g + F, :], basis[:, k, :],
                                      prod[:, (k * STREAMS + g) % G_BUFS, :], start=k == 0, stop=k == KCH - 1,
                                      tile_position=(0, F * g))
                last_.then_inc(msg_done, 1)

            def score_sum(s):
                wait_step(pe, s, score_ready)
                pe.matmul(bank[1][:, :], ones_blk[:, :], score, start=True, stop=True).then_inc(sum_done, 1)

            def compose(s):
                wait_step(pe, s, onehot_ready)
                wait_step(pe, s, score_ready, lag=1)
                wait_step(pe, s, weight_ready, lag=1)
                for g in range(STREAMS):
                    o = 64 * (g % 2)
                    last_ = pe.matmul(bank[g // 2][o:o + 64, :], comp_lhs[:, :], onehot[:, s.slot(2), g, :],
                                      start=True, stop=True, tile_position=(0, o))
                last_.then_inc(comp_done, 1)

            def relate(s):
                wait_step(pe, s, onehot_ready)
                wait_step(pe, s, query_ready, lag=1)
                for q in range(PARTS):
                    for g in range(STREAMS):
                        last_ = pe.matmul(bank[5][F * g:F * g + F, :], rel_parts[:, q, 0:F],
                                          onehot[:, s.slot(2), g, :], start=q == 0, stop=q == PARTS - 1,
                                          tile_position=(0, F * g))
                last_.then_inc(rel_done, 1)

            def source_turn(s, g):
                if g == 0:
                    wait_in(pe, s, gathered[1], 16 * SLOTS)
                if g < 2:
                    wait_step(pe, s, comp_ready, each=2, more=g - 1)
                else:
                    wait_step(pe, s, x_ready[1], each=STREAMS, more=g - 2 - 3)
                out = bank[g % 2][:, :].rearrange("p (n j) -> p j n", j=TILES)
                for j in range(TILES):
                    last_ = pe.transpose(out[:, j, :], xg[:, s.slot(2), j * STREAMS + g, :], ident[:, :])
                last_.then_inc(x_turned[1], 1)

            def find_key(s):
                wait_step(pe, s, x_ready[1], each=STREAMS)
                for g in range(STREAMS):
                    last_ = pe.matmul(bank[0][F * g:F * g + F, :], a1w[:, :], x4[:, s.slot(2), g, :],
                                      start=True, stop=True, tile_position=(0, F * g))
                last_.then_inc(key_done, 1)

            def step1(s):
                ahead, behind = s.plus(1), s.plus(-1)
                turns, key, summed = LATE_TURNS if s.known and s.at >= STEPS - 2 else TURNS
                for n in range(SLOTS):
                    coef(s, n)
                    if n == summed:
                        score_sum(s)
                    if n == 1 and behind.exists():
                        messages(behind, KCH - 1)
                    if n in (7, 10, 14):
                        messages(s, (n - 7 + 1) // 3)
                    if n == 12 and behind.exists():
                        scan_turn(1, behind, 4)
                    if ahead.exists():
                        if n == 2:
                            relate(ahead)
                        if n == 3:
                            compose(ahead)
                        if n == 4:
                            wait_step(pe, s, o_ready[1], lag=2)
                            spread_turn(1, ahead, 4)
                        if n in turns:
                            source_turn(ahead, turns.index(n))
                        if n == key:
                            find_key(ahead)

            first_step = Step(4, 0, 0)
            relate(first_step)
            compose(first_step)
            spread_turn(1, first_step, 4)
            for g in range(STREAMS):
                source_turn(first_step, g)
            find_key(first_step)
            run_steps(pe, step1, 4)
            messages(Step(4, 0, STEPS - 1), KCH - 1)
            scan_turn(1, Step(4, 0, STEPS - 1), 4)

            for c in range(CHUNKS):
                pe.wait_ge(picked, c + 1)
                if c > 0:
                    pe.wait_ge(added, c)
                node_map(CHUNKS + c, y[:, 0:CHUNK, :], self_w)




def _blocks(a, n):
    r, c = a.shape
    out = np.zeros((n * r, n * c), a.dtype)
    for i in range(n):
        out[i * r:(i + 1) * r, i * c:(i + 1) * c] = a
    return out


def kernel(x, src, dst, edge_attr_32, edge_type_86, L0_gnn_W1, L0_gnn_b1, L0_gnn_W2, L0_gnn_b2,
           L1_gnn_weight, L1_gnn_w_comp, L1_gnn_self_loop_weight, L1_gnn_A1_w, L1_gnn_A1_b,
           L1_gnn_A2_w, L1_gnn_A2_b, L1_gnn_rel_emb):
    from concourse import bacc
    from concourse.bass_utils import run_bass_kernel_spmd

    f32 = np.float32
    xs, src, dst, types, attr = (np.asarray(a) for a in (x, src, dst, edge_type_86, edge_attr_32))
    pad = EDGES - N_EDGES
    x_pad = np.concatenate([xs, np.zeros((NODES - N_NODES, F), f32)])
    src_pad = np.concatenate([src, np.zeros(pad, src.dtype)])
    dst_pad = np.concatenate([dst, np.full(pad, NODES, dst.dtype)])
    type_pad = np.concatenate([types, np.zeros(pad, types.dtype)])
    attr_pad = np.concatenate([attr, np.zeros((pad, F), f32)])
    prev = np.concatenate([np.full(1, -1, dst.dtype), dst_pad[:-1]])

    W1 = np.asarray(L0_gnn_W1).reshape(3, F, HID)
    w1 = np.zeros((P, 3, 2, P), f32)
    w2 = np.zeros((P, 2, P), f32)
    for g in range(STREAMS):
        q, o = g // 2, HID * (g % 2)
        w1[F * g:F * g + F, :, q, o:o + HID] = W1.transpose(1, 0, 2)
        w2[o:o + HID, q, F * g:F * g + F] = np.asarray(L0_gnn_W2)
    sel = np.zeros((2, 64, 2, KCH, 4, F), f32)
    for half in range(2):
        for q in range(PARTS):
            for k in range(KCH):
                for b in range(4):
                    sel[half, q * BASES + 4 * k + b, half, k, b, :] = 1.0
    rel = np.zeros((P, F + BASES), f32)
    n_types = np.asarray(L1_gnn_rel_emb).shape[0]
    rel[:n_types, :F] = np.asarray(L1_gnn_rel_emb)
    rel[:n_types, F:] = np.asarray(L1_gnn_w_comp)
    nodes = (np.arange(P)[:, None] * NODE_COLS + np.arange(NODE_COLS + 1)[None, :]).astype(f32)

    arrays = {
        "x_dram": x_pad,
        "x_nodes": x_pad.reshape(P, NODE_COLS, F),
        "src_t": src_pad.reshape(STREAMS, STEPS, P, TILES).transpose(1, 2, 3, 0).reshape(STEPS, P, SLOTS),
        "dst_rows": dst_pad.reshape(P, ROW),
        "prev_rows": prev.reshape(P, ROW),
        "type_rows": type_pad.reshape(P, ROW),
        "block_rows": np.concatenate([np.full(ROW, SHIFT, dst.dtype), dst_pad[:-ROW]]).reshape(P, ROW),
        "head": dst_pad[::ROW].reshape(P, 1),
        "step_98": np.tile(nodes[:, 0], (P, 1)),
        "minus_col": np.tile(-np.arange(NODE_COLS + 1, dtype=f32), (P, 1)),
        "heads4": dst_pad[::STREAM].reshape(STREAMS, 1),
        "edge_t": attr_pad.reshape(STREAMS, STREAM, F).transpose(0, 2, 1).reshape(P, STREAM),
        "w1": w1,
        "w2": w2,
        "b1": np.tile(np.asarray(L0_gnn_b1), 2).reshape(P, 1),
        "b2": np.asarray(L0_gnn_b2),
        "a1w": np.concatenate([np.asarray(L1_gnn_A1_w).T, np.zeros((P - F, F), f32)]),
        "a1b": np.tile(np.asarray(L1_gnn_A1_b), 4).reshape(P, 1),
        "a2w": _blocks(np.asarray(L1_gnn_A2_w).T, 4),
        "a2b": np.asarray(L1_gnn_A2_b),
        "self_w": _blocks(np.asarray(L1_gnn_self_loop_weight), 4),
        "basis": np.asarray(L1_gnn_weight).reshape(KCH, P, F).transpose(1, 0, 2),
        "rel": rel,
        "ident": np.eye(P, dtype=f32),
        "ones_blk": _blocks(np.ones((F, F), f32), 4),
        "sel": sel.reshape(P, 2 * KCH, P),
        "row_id": np.arange(P, dtype=f32).reshape(P, 1),
        "node_less": nodes - SHIFT,
        "node_half": nodes - (SHIFT + 0.5),
        "spare_id": nodes[:, :NODE_COLS] + EDGES,
    }
    arrays = {k: np.ascontiguousarray(a) for k, a in arrays.items()}

    nc = bacc.Bacc("TRN2", target_bir_lowering=False, num_devices=1)
    t = {k: nc.dram_tensor("in_" + k, a.shape, mybir.dt.from_np(a.dtype), kind="ExternalInput").ap()
         for k, a in arrays.items()}
    t["out"] = nc.dram_tensor("out", (N_NODES, F), fp32, kind="ExternalOutput").ap()
    build(nc, t)
    r = run_bass_kernel_spmd(nc, [{"in_" + k: a for k, a in arrays.items()}], core_ids=[0])
    return r.results[0]["out"]
```
